# Optimizing a Trainium2 kernel written in Bass

```python
import numpy as np
import jax
import jax.numpy as jnp

def _softmax(x, axis=-1):
    return jax.nn.softmax(x, axis=axis)

def _gelu(x):
    return jax.nn.gelu(x, approximate=True)

def _silu(x):
    return jax.nn.silu(x)

def _sigmoid(x):
    return jax.nn.sigmoid(x)

def _layernorm(x, axis=-1, eps=1e-05):
    m = jnp.mean(x, axis=axis, keepdims=True)
    v = jnp.var(x, axis=axis, keepdims=True)
    return (x - m) / jnp.sqrt(v + eps)

def _scatter_add(tgt, idx, src, axis=0):
    return tgt.at[idx].add(src)

def _segment_sum(src, seg, n):
    return jax.ops.segment_sum(src, seg, n)
kernel_name = 'mk_recurrent_d1_jaxref_r8_69c168'

def setup_inputs(seed: int=0):
    np.random.seed(seed)
    _w = jnp.asarray

    def _L0_attn_setup():
        import jax, jax.numpy as jnp
        import numpy as np
        DIM = 128
        HEADS = 16
        HEAD_DIM = DIM // HEADS
        B, S = (4, 512)
        key = jax.random.key(seed)
        ks = jax.random.split(key, 8)
        sc = 1.0 / np.sqrt(DIM)
        return {'x': jax.random.normal(ks[0], (B, S, DIM), dtype=jnp.float32), 'Wq': jax.random.normal(ks[1], (DIM, DIM), dtype=jnp.float32) * sc, 'Wk': jax.random.normal(ks[2], (DIM, DIM), dtype=jnp.float32) * sc, 'Wv': jax.random.normal(ks[3], (DIM, DIM), dtype=jnp.float32) * sc, 'Wp': jax.random.normal(ks[4], (DIM, DIM), dtype=jnp.float32) * sc, 'bp': jnp.zeros((DIM,), dtype=jnp.float32), 'conv_w': jax.random.normal(ks[5], (DIM, 3), dtype=jnp.float32) * (1.0 / np.sqrt(3.0)), 'conv_b': jnp.zeros((DIM,), dtype=jnp.float32)}
    _L0_attn_in = _L0_attn_setup()

    def _L0_ffn_setup():
        import jax, jax.numpy as jnp
        import numpy as np
        DIM = 128
        DEPTH = 6
        HEADS = 16
        DIM_HEAD = 64
        WINDOW = 32
        INNER = HEADS * DIM_HEAD
        DIM_INNER = int(DIM * 4 * 2 / 3)
        QK_SCALE = 8.0

        def shift_tokens(t):
            a, s = jnp.split(t, 2, -1)
            s = jnp.pad(s, ((0, 0), (1, 0), (0, 0)))[:, :-1]
            return jnp.concatenate([a, s], -1)

        def l2norm(t):
            return t / jnp.maximum(jnp.linalg.norm(t, axis=-1, keepdims=True), 1e-12)

        def rotate_half(x):
            x1, x2 = jnp.split(x, 2, -1)
            return jnp.concatenate([-x2, x1], -1)

        def rotary_tables(n):
            half = jnp.arange(0, DIM_HEAD, 2, dtype=jnp.float32)
            inv_freq = 1.0 / 10000.0 ** (half / DIM_HEAD)
            t = jnp.arange(n, dtype=jnp.float32)
            freqs = t[:, None] * inv_freq[None, :]
            freqs = jnp.concatenate([freqs, freqs], -1)
            base_scale = (half + 0.4 * DIM_HEAD) / (1.4 * DIM_HEAD)
            power = (t - n // 2) / (WINDOW // 2)
            scale = base_scale[None, :] ** power[:, None]
            scale = jnp.concatenate([scale, scale], -1)
            return (freqs, scale)

        def local_attention(q, k, v):
            b, h, n, d = q.shape
            w = WINDOW
            nw = n // w
            bq = q.reshape(b, h, nw, w, d)
            bk = k.reshape(b, h, nw, w, d)
            bv = v.reshape(b, h, nw, w, d)

            def look(t):
                p = jnp.pad(t, ((0, 0), (0, 0), (1, 0), (0, 0), (0, 0)))
                return jnp.concatenate([p[:, :, :nw], p[:, :, 1:]], axis=3)
            bk2, bv2 = (look(bk), look(bv))
            seq = jnp.arange(n).reshape(nw, w)
            seq_p = jnp.pad(seq, ((1, 0), (0, 0)), constant_values=-1)
            jt = jnp.concatenate([seq_p[:nw], seq_p[1:]], axis=1)
            it = seq[:, :, None]
            jb = jt[:, None, :]
            mask = (it < jb) | (it > jb + w) | (jb == -1)
            sim = jnp.einsum('bhwie,bhwje->bhwij', bq, bk2) * QK_SCALE
            sim = jnp.where(mask, -jnp.finfo(sim.dtype).max, sim)
            attn = jax.nn.softmax(sim, -1)
            out = jnp.einsum('bhwij,bhwje->bhwie', attn, bv2)
            return out.reshape(b, h, n, d)

        def attn_layer(x, Wqkv, qs, ksc, Wo):
            b, n, _ = x.shape
            qkv = x @ Wqkv
            q, k, v = jnp.split(qkv, 3, -1)
            sh = lambda t: t.reshape(b, n, HEADS, DIM_HEAD).transpose(0, 2, 1, 3)
            q, k, v = (sh(q), sh(k), sh(v))
            q = l2norm(q) * qs
            k = l2norm(k) * ksc
            freqs, scale = rotary_tables(n)
            cos, sin = (jnp.cos(freqs), jnp.sin(freqs))
            q = q * cos * scale + rotate_half(q) * sin * scale
            inv = 1.0 / scale
            k = k * cos * inv + rotate_half(k) * sin * inv
            out = local_attention(q, k, v)
            out = out.transpose(0, 2, 1, 3).reshape(b, n, INNER)
            return out @ Wo

        def ffn_layer(x, g, bln, W1, b1, W2, b2):
            mu = x.mean(-1, keepdims=True)
            var = ((x - mu) ** 2).mean(-1, keepdims=True)
            xn = (x - mu) / jnp.sqrt(var + 1e-05) * g + bln
            hg = xn @ W1 + b1
            a, gate = jnp.split(hg, 2, -1)
            return a * jax.nn.gelu(gate, approximate=False) @ W2 + b2
        key = jax.random.key(seed)
        ks = jax.random.split(key, 8)
        B, N = (2, 256)
        init = lambda k, shape: jax.random.normal(k, shape, jnp.float32) * 0.02
        return {'x': jax.random.normal(ks[0], (B, N, DIM), jnp.float32), 'Wqkv': init(ks[1], (DEPTH, DIM, 3 * INNER)), 'q_scale': jnp.ones((DEPTH, DIM_HEAD), jnp.float32), 'k_scale': jnp.ones((DEPTH, DIM_HEAD), jnp.float32), 'Wo': init(ks[2], (DEPTH, INNER, DIM)), 'ln_g': jnp.ones((DEPTH, DIM), jnp.float32), 'ln_b': jnp.zeros((DEPTH, DIM), jnp.float32), 'W1': init(ks[3], (DEPTH, DIM, 2 * DIM_INNER)), 'b1': jnp.zeros((DEPTH, 2 * DIM_INNER), jnp.float32), 'W2': init(ks[4], (DEPTH, DIM_INNER, DIM)), 'b2': jnp.zeros((DEPTH, DIM), jnp.float32)}
    _L0_ffn_in = _L0_ffn_setup()
    _d = {'L0_attn_x': _L0_attn_in['x'], 'L0_attn_Wq': _L0_attn_in['Wq'], 'L0_attn_Wk': _L0_attn_in['Wk'], 'L0_attn_Wv': _L0_attn_in['Wv'], 'L0_attn_Wp': _L0_attn_in['Wp'], 'L0_attn_bp': _L0_attn_in['bp'], 'L0_attn_conv_w': _L0_attn_in['conv_w'], 'L0_attn_conv_b': _L0_attn_in['conv_b'], 'L0_ffn_Wqkv': _L0_ffn_in['Wqkv'], 'L0_ffn_q_scale': _L0_ffn_in['q_scale'], 'L0_ffn_k_scale': _L0_ffn_in['k_scale'], 'L0_ffn_Wo': _L0_ffn_in['Wo'], 'L0_ffn_ln_g': _L0_ffn_in['ln_g'], 'L0_ffn_ln_b': _L0_ffn_in['ln_b'], 'L0_ffn_W1': _L0_ffn_in['W1'], 'L0_ffn_b1': _L0_ffn_in['b1'], 'L0_ffn_W2': _L0_ffn_in['W2'], 'L0_ffn_b2': _L0_ffn_in['b2']}
    _x0 = _d['L0_attn_x']
    _d['L0_attn_x'] = jax.random.normal(jax.random.fold_in(jax.random.key(seed), 1), (8, 256, 128), dtype=_x0.dtype)
    del _x0
    return _d

def reference(L0_attn_x, L0_attn_Wq, L0_attn_Wk, L0_attn_Wv, L0_attn_Wp, L0_attn_bp, L0_attn_conv_w, L0_attn_conv_b, L0_ffn_Wqkv, L0_ffn_q_scale, L0_ffn_k_scale, L0_ffn_Wo, L0_ffn_ln_g, L0_ffn_ln_b, L0_ffn_W1, L0_ffn_b1, L0_ffn_W2, L0_ffn_b2):

    def _L0_attn_ref(x, Wq, Wk, Wv, Wp, bp, conv_w, conv_b):
        import jax, jax.numpy as jnp
        import numpy as np
        DIM = 128
        HEADS = 16
        HEAD_DIM = DIM // HEADS
        B, S = (4, 512)
        b, s, d = x.shape

        def split_heads(t):
            return t.reshape(b, s, HEADS, HEAD_DIM).transpose(0, 2, 1, 3)
        q = split_heads(x @ Wq.T)
        k = split_heads(x @ Wk.T)
        v = split_heads(x @ Wv.T)
        q = jax.nn.elu(q) + 1.0
        k = jax.nn.elu(k) + 1.0
        kv_state = jnp.einsum('bhnd,bhne->bhde', k, v)
        k_state = k.sum(axis=2)
        attn_out = jnp.einsum('bhnd,bhde->bhne', q, kv_state)
        denom = jnp.maximum(jnp.einsum('bhnd,bhd->bhn', q, k_state), 1e-06)[..., None]
        attn_out = (attn_out / denom).transpose(0, 2, 1, 3).reshape(b, s, d)
        xp = jnp.pad(x, ((0, 0), (1, 1), (0, 0)))
        local = xp[:, :-2, :] * conv_w[:, 0] + xp[:, 1:-1, :] * conv_w[:, 1] + xp[:, 2:, :] * conv_w[:, 2] + conv_b
        return (attn_out + local) @ Wp.T + bp

    def _L0_ffn_ref(x, Wqkv, q_scale, k_scale, Wo, ln_g, ln_b, W1, b1, W2, b2):
        import jax, jax.numpy as jnp
        import numpy as np
        DIM = 128
        DEPTH = 6
        HEADS = 16
        DIM_HEAD = 64
        WINDOW = 32
        INNER = HEADS * DIM_HEAD
        DIM_INNER = int(DIM * 4 * 2 / 3)
        QK_SCALE = 8.0

        def shift_tokens(t):
            a, s = jnp.split(t, 2, -1)
            s = jnp.pad(s, ((0, 0), (1, 0), (0, 0)))[:, :-1]
            return jnp.concatenate([a, s], -1)

        def l2norm(t):
            return t / jnp.maximum(jnp.linalg.norm(t, axis=-1, keepdims=True), 1e-12)

        def rotate_half(x):
            x1, x2 = jnp.split(x, 2, -1)
            return jnp.concatenate([-x2, x1], -1)

        def rotary_tables(n):
            half = jnp.arange(0, DIM_HEAD, 2, dtype=jnp.float32)
            inv_freq = 1.0 / 10000.0 ** (half / DIM_HEAD)
            t = jnp.arange(n, dtype=jnp.float32)
            freqs = t[:, None] * inv_freq[None, :]
            freqs = jnp.concatenate([freqs, freqs], -1)
            base_scale = (half + 0.4 * DIM_HEAD) / (1.4 * DIM_HEAD)
            power = (t - n // 2) / (WINDOW // 2)
            scale = base_scale[None, :] ** power[:, None]
            scale = jnp.concatenate([scale, scale], -1)
            return (freqs, scale)

        def local_attention(q, k, v):
            b, h, n, d = q.shape
            w = WINDOW
            nw = n // w
            bq = q.reshape(b, h, nw, w, d)
            bk = k.reshape(b, h, nw, w, d)
            bv = v.reshape(b, h, nw, w, d)

            def look(t):
                p = jnp.pad(t, ((0, 0), (0, 0), (1, 0), (0, 0), (0, 0)))
                return jnp.concatenate([p[:, :, :nw], p[:, :, 1:]], axis=3)
            bk2, bv2 = (look(bk), look(bv))
            seq = jnp.arange(n).reshape(nw, w)
            seq_p = jnp.pad(seq, ((1, 0), (0, 0)), constant_values=-1)
            jt = jnp.concatenate([seq_p[:nw], seq_p[1:]], axis=1)
            it = seq[:, :, None]
            jb = jt[:, None, :]
            mask = (it < jb) | (it > jb + w) | (jb == -1)
            sim = jnp.einsum('bhwie,bhwje->bhwij', bq, bk2) * QK_SCALE
            sim = jnp.where(mask, -jnp.finfo(sim.dtype).max, sim)
            attn = jax.nn.softmax(sim, -1)
            out = jnp.einsum('bhwij,bhwje->bhwie', attn, bv2)
            return out.reshape(b, h, n, d)

        def attn_layer(x, Wqkv, qs, ksc, Wo):
            b, n, _ = x.shape
            qkv = x @ Wqkv
            q, k, v = jnp.split(qkv, 3, -1)
            sh = lambda t: t.reshape(b, n, HEADS, DIM_HEAD).transpose(0, 2, 1, 3)
            q, k, v = (sh(q), sh(k), sh(v))
            q = l2norm(q) * qs
            k = l2norm(k) * ksc
            freqs, scale = rotary_tables(n)
            cos, sin = (jnp.cos(freqs), jnp.sin(freqs))
            q = q * cos * scale + rotate_half(q) * sin * scale
            inv = 1.0 / scale
            k = k * cos * inv + rotate_half(k) * sin * inv
            out = local_attention(q, k, v)
            out = out.transpose(0, 2, 1, 3).reshape(b, n, INNER)
            return out @ Wo

        def ffn_layer(x, g, bln, W1, b1, W2, b2):
            mu = x.mean(-1, keepdims=True)
            var = ((x - mu) ** 2).mean(-1, keepdims=True)
            xn = (x - mu) / jnp.sqrt(var + 1e-05) * g + bln
            hg = xn @ W1 + b1
            a, gate = jnp.split(hg, 2, -1)
            return a * jax.nn.gelu(gate, approximate=False) @ W2 + b2
        for i in range(DEPTH):
            x = attn_layer(shift_tokens(x), Wqkv[i], q_scale[i], k_scale[i], Wo[i]) + x
            x = ffn_layer(shift_tokens(x), ln_g[i], ln_b[i], W1[i], b1[i], W2[i], b2[i]) + x
        return x
    x = L0_attn_x
    xn = _layernorm(x, axis=-1)
    s = _L0_attn_ref(xn, L0_attn_Wq, L0_attn_Wk, L0_attn_Wv, L0_attn_Wp, L0_attn_bp, L0_attn_conv_w, L0_attn_conv_b)
    g = _silu(_L0_ffn_ref(xn, L0_ffn_Wqkv, L0_ffn_q_scale, L0_ffn_k_scale, L0_ffn_Wo, L0_ffn_ln_g, L0_ffn_ln_b, L0_ffn_W1, L0_ffn_b1, L0_ffn_W2, L0_ffn_b2))
    x = x + s * g
    return x

_drawn_inputs = setup_inputs


def setup_inputs(seed=0):
    import zlib

    import numpy as np

    out = dict(_drawn_inputs(seed))
    spreads = {'L0_attn_bp': (0.0, 0.1),
     'L0_attn_conv_b': (0.0, 0.1),
     'L0_ffn_q_scale': (1.0, 0.6),
     'L0_ffn_k_scale': (1.0, 0.6),
     'L0_ffn_ln_g': (1.0, 0.6),
     'L0_ffn_ln_b': (0.0, 0.8),
     'L0_ffn_b1': (0.0, 0.8),
     'L0_ffn_b2': (0.0, 0.1)}
    factors = {'L0_attn_Wq': 6.454, 'L0_attn_Wk': 3.438, 'L0_ffn_W1': 3.175, 'L0_ffn_W2': 3.13}
    for name, (base, spread) in spreads.items():
        noise = np.random.default_rng([zlib.crc32(name.encode()), seed]).standard_normal(out[name].shape)
        drawn = base * np.exp(spread * noise) if base else spread * noise
        out[name] = jnp.asarray(drawn.astype(out[name].dtype))
    for name, factor in factors.items():
        out[name] = (out[name] * factor).astype(out[name].dtype)
    return out
```

```python
from contextlib import ExitStack

import numpy as np

import concourse.bass as bass
from concourse import mybir

F32 = mybir.dt.float32
F32R = mybir.dt.float32r
BF16 = mybir.dt.bfloat16
ALU = mybir.AluOpType
ACT = mybir.ActivationFunctionType
AX = mybir.AxisListType.X

P = 128
BATCHES, TOKENS, DIM = 8, 256, 128
DEPTH, HEADS, HEAD, WINDOW = 6, 16, 64, 32
INNER = HEADS * HEAD
FF = DIM * 4 * 2 // 3
QK_SCALE = 8.0
ALL = BATCHES * TOKENS
TILES = TOKENS // P
OCTET = 8 * HEAD
PAIRS = OCTET // P
CHUNKS = INNER // P
UNITS = 4
STEPS = DEPTH * BATCHES
SLICES = 8
SLICE = 3 * INNER // SLICES
FF_ROWS = [min(P, FF - P * i) for i in range((FF + P - 1) // P)]
FF_N = len(FF_ROWS)
MASKED = -1.0e30
SQ_SCALE = 2.0 ** 16
LN_EPS = 1e-5
LINEAR_HEAD = DIM // HEADS

PRE_DVE = ["center", "var", "newton_a", "newton_b", "rstd", "xn", "keep", "q_neg", "k_neg", "v_copy",
           "conv_mid", "conv_left", "conv_right", "q_feat", "k_feat", "kv_state", "k_state", "den",
           "den_inv", "attn", "mix"]
PRE_ACT = ["square", "ln", "rsqrt", "q_exp", "k_exp", "out"]
PRE_PE = ["mean", "var", "qkv", "state", "read", "out"]


def build(nc, x, wq, wk, wv, wp, bp, conv_w, conv_b, wqkv, q_scale, k_scale, wo, ln_g, ln_b, w1, b1, w2, b2,
          rotary, masks, eye, head_block, out):
    with ExitStack() as ctx:
        def sb(name, shape, dt=F32):
            return ctx.enter_context(nc.sbuf_tensor(name, shape, dt))

        def bank(name):
            return ctx.enter_context(nc.psum_tensor(name, [P, 512], F32))

        def sem(name):
            return ctx.enter_context(nc.semaphore(name))

        x_in = sb("x_in", [P, ALL])
        x_run = sb("x_run", [P, ALL])
        s_out = sb("s_out", [P, ALL])
        w_hi = sb("w_hi", [P, 2 * 3 * INNER], F32R)
        w_lo = sb("w_lo", [P, 2 * 3 * INNER], F32R)
        w_raw = sb("w_raw", [P, 2 * SLICE])
        wo_sb = sb("wo_sb", [P, CHUNKS, DIM])
        w1_sb = sb("w1_sb", [P, 2 * FF])
        w2_sb = sb("w2_sb", [P, FF_N, DIM])
        b1_sb = sb("b1_sb", [P, 2 * FF_N])
        b2_sb = sb("b2_sb", [P, 1])
        ln_sb = sb("ln_sb", [P, 2])
        table = sb("table", [P, DEPTH * 4 * TILES * HEAD])
        ident = sb("ident", [P, P])
        ident_b = sb("ident_b", [P, P], BF16)
        mask_b = sb("mask_b", [P, TILES, 512], BF16)
        mean_w = sb("mean_w", [P, P])
        xs_hi = sb("xs_hi", [P, TOKENS], F32R)
        xs_lo = sb("xs_lo", [P, TOKENS], F32R)
        squares = sb("squares", [P, 2, 2 * OCTET])
        ssq = sb("ssq", [P, 2, 16])
        ssq_c = sb("ssq_c", [P, 2, 16])
        ssq_ln = sb("ssq_ln", [P, 2, 16])
        rn_0 = sb("rn_0", [P, 2, 16])
        rn_a = sb("rn_a", [P, 2, 16])
        rn_b = sb("rn_b", [P, 2, 16])
        rnorm = sb("rnorm", [P, 2, 16])
        qk = sb("qk", [P, 2, 2, OCTET])
        qk_rot = sb("qk_rot", [P, 2, 2, OCTET])
        q_bd = sb("q_bd", [P, 2, PAIRS * 4, 2, WINDOW])
        k_t = sb("k_t", [P, 2, PAIRS, WINDOW + TOKENS])
        prob = sb("prob", [P, 2, OCTET])
        p_bd = sb("p_bd", [P, 2, PAIRS * 4, 2, WINDOW])
        row_max = sb("row_max", [P, 2, 8])
        row_sum = sb("row_sum", [P, 2, 8])
        row_inv = sb("row_inv", [P, 2, 8])
        v_own = sb("v_own", [P, UNITS, OCTET])
        v_back = sb("v_back", [P, UNITS, OCTET])
        attn_t = sb("attn_t", [P, CHUNKS, TOKENS])
        x_mid = sb("x_mid", [P, 2 * TOKENS])
        xs = sb("xs", [P, TOKENS])
        xc = sb("xc", [P, TOKENS])
        lnt = sb("lnt", [P, 6, TOKENS])
        xn = sb("xn", [P, TOKENS])
        ff_a = sb("ff_a", [P, FF_N, TOKENS])
        ff_g = sb("ff_g", [P, FF_N, TOKENS])

        pre = qk_rot[:].rearrange("p a b c -> p (a b c)")
        wqt, wkvt, wpt = attn_t[:, 0, 0:P], attn_t[:, 1, :], attn_t[:, 2, 0:P]
        bp_sb, conv_sb, convb_sb = attn_t[:, 3, 0:1], attn_t[:, 3, 1:4], attn_t[:, 3, 4:5]
        block_sb = attn_t[:, 4, 0:P]
        ones = attn_t[:, 5, 0:P]
        qsc = attn_t[:, 6:8, :].rearrange("p a b -> p (a b)")
        ksc = prob[:, 0, 0:DEPTH * HEAD]
        rot_sb = squares[:, 0, 0:4 * TILES * HEAD]
        mask_f = qk[:, 0].rearrange("p a b -> p (a b)")

        ps_q, ps_k, ps_v, ps_tq, ps_tk, ps_s, ps_pt, ps_o = (
            bank(n) for n in ("ps_q", "ps_k", "ps_v", "ps_tq", "ps_tk", "ps_s", "ps_pt", "ps_o"))

        x_loaded, consts_loaded, raw_loaded, out_stored = sem("x_loaded"), sem("consts_loaded"), sem("raw_loaded"), sem("out_stored")
        wo_loaded, w1_loaded, w2_loaded, ln_loaded = sem("wo_loaded"), sem("w1_loaded"), sem("w2_loaded"), sem("ln_loaded")
        v_shifted = [sem(f"v_shifted_{j}") for j in range(UNITS)]
        pool_ready, zeros_ready = sem("pool_ready"), sem("zeros_ready")
        consts_ready, w_split, w_rounded = sem("consts_ready"), sem("w_split"), sem("w_rounded")
        pre_pe, pre_act, pre_dve = sem("pre_pe"), sem("pre_act"), sem("pre_dve")
        x_ready, xs_rounded, xs_ready = sem("x_ready"), sem("xs_rounded"), sem("xs_ready")
        q_done, k_done, v_done = sem("q_done"), sem("k_done"), sem("v_done")
        tq_done, tk_done, pt_done, s_done, o_done = sem("tq_done"), sem("tk_done"), sem("pt_done"), sem("s_done"), sem("o_done")
        wo_done, mean_done, var_done, ff1_done, ff2_done = sem("wo_done"), sem("mean_done"), sem("var_done"), sem("ff1_done"), sem("ff2_done")
        q_squared, k_squared, v_copied, q_turned, k_turned, p_turned, exp_done, attn_copied = (
            sem(n) for n in ("q_squared", "k_squared", "v_copied", "q_turned", "k_turned", "p_turned", "exp_done", "attn_copied"))
        ssq_logged, rn_started, ln_squared, ln_logged, ln_started, ff1_copied, gelu_done, silu_exp = (
            sem(n) for n in ("ssq_logged", "rn_started", "ln_squared", "ln_logged", "ln_started", "ff1_copied", "gelu_done", "silu_exp"))
        q_scaled, k_scaled, ssq_done, ssq_clamped, rn_step, rnorm_done = (
            sem(n) for n in ("q_scaled", "k_scaled", "ssq_done", "ssq_clamped", "rn_step", "rnorm_done"))
        max_done, sub_done, sum_done, inv_done = sem("max_done"), sem("sub_done"), sem("sum_done"), sem("inv_done")
        mid_done, centered, var_ready, ln_step, xn_ready, ff_mixed, final, final_step = (
            sem(n) for n in ("mid_done", "centered", "var_ready", "ln_step", "xn_ready", "ff_mixed", "final", "final_step"))
        q_added, k_added, q_normed, k_normed, p_normed = (
            sem(n) for n in ("q_added", "k_added", "q_normed", "k_normed", "p_normed"))

        CONSTS = 16 * 16

        def live(u):
            return not isinstance(u, int) or 0 <= u < UNITS * STEPS

        def live_batch(m):
            return not isinstance(m, int) or 0 <= m < STEPS

        def wait(eng, s, value):
            if not isinstance(value, int) or value > 0:
                eng.wait_ge(s, value)

        def columns(m):
            if isinstance(m, int):
                return slice(m % BATCHES * TOKENS, m % BATCHES * TOKENS + TOKENS)
            return bass.ds(m % BATCHES * TOKENS, TOKENS)

        def span(start, size):
            return slice(start, start + size) if isinstance(start, int) else bass.ds(start, size)

        def iterations(eng, body, switch=2, end=STEPS):
            body(0)
            body(1)
            if switch != 2:
                with eng.Fori(2, switch) as n:
                    body(n)
            with eng.Fori(max(switch, 2), end) as n:
                body(n, switch == 2)
            body(STEPS)
            body(STEPS + 1)

        block = ctx.enter_context(nc.Block())

        @block.sync
        def _(sp):
            for b in range(BATCHES):
                sp.dma_start(x_in[:, columns(b)], x[:, columns(b)]).then_inc(x_loaded, 16)
            for dst, src in ((rot_sb, rotary), (qsc[:, 0:DEPTH * HEAD], q_scale.partition_broadcast(P)),
                             (ksc, k_scale.partition_broadcast(P)), (wqt, wq), (wkvt[:, 0:P], wk),
                             (wkvt[:, P:2 * P], wv), (wpt, wp), (bp_sb, bp), (conv_sb, conv_w), (convb_sb, conv_b),
                             (block_sb, head_block), (ident[:], eye), (mask_f, masks)):
                sp.dma_start(dst, src).then_inc(consts_loaded, 16)

            def load_slice(k):
                half = k % 2 * SLICE
                if isinstance(k, int):
                    wait(sp, raw_loaded, 16 * k)
                    wait(sp, w_split, k - 1)
                else:
                    sp.wait_ge(w_split, k)
                sp.dma_start(w_raw[:, span(half, SLICE)],
                             wqkv[k] if isinstance(k, int) else wqkv[bass.ds(k, 1)].rearrange("a p c -> (a p) c")
                             ).then_inc(raw_loaded, 16)

            def layer_of(t, l):
                return t[l] if isinstance(l, int) else t[bass.ds(l, 1)].rearrange("a p c -> (a p) c")

            def load_wo(l):
                wait(sp, wo_done, BATCHES * l)
                sp.dma_start(wo_sb[:].rearrange("p c d -> p (c d)"), layer_of(wo, l)).then_inc(wo_loaded, 16)

            def load_ln(l):
                wait(sp, xn_ready, BATCHES * l)
                sp.dma_start(ln_sb[:, 0:1], layer_of(ln_g, l)).then_inc(ln_loaded, 16)
                sp.dma_start(ln_sb[:, 1:2], layer_of(ln_b, l)).then_inc(ln_loaded, 16)

            def load_w1(l):
                wait(sp, ff1_copied, FF_N * BATCHES * l)
                sp.dma_start(w1_sb[:], layer_of(w1, l)).then_inc(w1_loaded, 16)
                sp.dma_start(b1_sb[:], layer_of(b1, l)).then_inc(w1_loaded, 16)

            def load_w2(l):
                if not isinstance(l, int) or l > 0:
                    sp.wait_ge(x_ready, BATCHES + BATCHES * l)
                sp.dma_start(w2_sb[:].rearrange("p c d -> p (c d)"), layer_of(w2, l)).then_inc(w2_loaded, 16)
                sp.dma_start(b2_sb[:], layer_of(b2, l)).then_inc(w2_loaded, 16)

            def shift_v(n, j):
                wait(sp, v_copied, UNITS * n + j + 1)
                sp.dma_start(v_back[WINDOW:P, j, :], v_own[0:P - WINDOW, j, :]).then_inc(v_shifted[j], 16)
                if j % 2:
                    sp.dma_start(v_back[0:WINDOW, j, :], v_own[P - WINDOW:P, j - 1, :]).then_inc(v_shifted[j], 16)

            for k in range(2):
                load_slice(k)
            for load in (load_wo, load_ln, load_w1, load_w2):
                load(0)
            for k in range(2, SLICES):
                load_slice(k)

            def body(n, b=3, l=0, slices=True):
                if slices:
                    load_slice(n + SLICES)
                for j in range(UNITS):
                    shift_v(n, j)
                    if b == 0 and j == 3:
                        load_wo(l)
                    if b == 1 and j == 0:
                        load_ln(l)
                    if b == 1 and j == 2:
                        load_w1(l)
                    if b == 2 and j == 0:
                        load_w2(l)

            body(0)
            body(1)
            with sp.Fori(2, BATCHES) as n:
                body(n)
            with sp.Fori(1, DEPTH - 1) as l:
                body(l * BATCHES, 0, l)
                body(l * BATCHES + 1, 1, l)
                body(l * BATCHES + 2, 2, l)
                with sp.Fori(3, BATCHES) as b:
                    body(l * BATCHES + b)
            n = (DEPTH - 1) * BATCHES
            body(n, 0, DEPTH - 1, slices=False)
            body(n + 1, 1, DEPTH - 1, slices=False)
            body(n + 2, 2, DEPTH - 1, slices=False)
            with sp.Fori(n + 3, STEPS) as n:
                body(n, slices=False)
            for b in range(BATCHES):
                wait(sp, final, b + 1)
                sp.dma_start(out[:, columns(b)], s_out[:, columns(b)]).then_inc(out_stored, 16)
            sp.wait_ge(out_stored, 16 * BATCHES)

        @block.gpsimd
        def _(pool):
            nc.gpsimd.memset(q_bd[:], 0.0)
            nc.gpsimd.memset(p_bd[:], 0.0)
            nc.gpsimd.memset(k_t[:, :, :, 0:WINDOW], 0.0)
            nc.gpsimd.memset(v_back[0:WINDOW, 0:UNITS:2, :], 0.0)
            nc.gpsimd.memset(ff_a[:], 0.0)
            nc.gpsimd.memset(ff_g[:], 0.0).then_inc(zeros_ready, 1)

            def heads(t):
                return t.rearrange("p (h d) -> p h d", d=HEAD)

            def normalise(n, j):
                u = UNITS * n + j
                s = j % 2
                for i, scaled, added in ((0, q_scaled, q_added), (1, k_scaled, k_added)):
                    pool.wait_ge(scaled, u + 1)
                    nc.gpsimd.tensor_tensor(qk[:, s, i, :], qk[:, s, i, :], qk_rot[:, s, i, :],
                                            ALU.add).then_inc(added, 1)
                pool.wait_ge(rnorm_done, u + 1)
                for i, added, normed in ((0, q_added, q_normed), (1, k_added, k_normed)):
                    pool.wait_ge(added, u + 1)
                    nc.gpsimd.tensor_tensor(heads(qk[:, s, i, :]), heads(qk[:, s, i, :]),
                                            rnorm[:, s, 8 * i:8 * i + 8].unsqueeze(2).to_broadcast([P, 8, HEAD]),
                                            ALU.mult).then_inc(normed, 1)

            def divide(u, s):
                pool.wait_ge(inv_done, u + 1)
                nc.gpsimd.tensor_tensor(heads(prob[:, s, :]), heads(prob[:, s, :]),
                                        row_inv[:, s, :].unsqueeze(2).to_broadcast([P, 8, HEAD]),
                                        ALU.mult).then_inc(p_normed, 1)

            def body(n, _=True):
                for j in range(UNITS):
                    u = UNITS * n + j
                    if live(u - 2):
                        divide(u - 2, j % 2)
                    if live(u):
                        normalise(n, j)

            iterations(pool, body)

        @block.tensor
        def _(pe):
            def mm(o, lhs, rhs, start, stop, **kw):
                return nc.tensor.matmul(o, lhs, rhs, start=start, stop=stop, **kw)

            pe.wait_ge(x_loaded, 16 * BATCHES)
            pe.wait_ge(consts_ready, 1)
            pe.wait_ge(pool_ready, 1)

            with pe.Fori(0, BATCHES) as b:
                def dve(step):
                    pe.wait_ge(pre_dve, b * len(PRE_DVE) + PRE_DVE.index(step) + 1)

                def act(step, ago=0):
                    pe.wait_ge(pre_act, b * len(PRE_ACT) + PRE_ACT.index(step) + 1)

                xn_b = pre[:, 0:TOKENS]
                mm(ps_q[:, 0:TOKENS], mean_w[:], x_in[:, columns(b)], True, True).then_inc(pre_pe, 1)
                act("square")
                mm(ps_k[:, 0:TOKENS], mean_w[:], pre[:, 512:768], True, True).then_inc(pre_pe, 1)
                dve("xn")
                mm(ps_tq[:, 0:TOKENS], wqt, xn_b, True, True)
                for t in range(TILES):
                    last = mm(ps_tk[:, 256 * t:256 * t + 256], pre[:, P * t:P * t + P], wkvt, True, True)
                last.then_inc(pre_pe, 1)
                dve("k_feat")
                kf = pre[:, 1024:1280]
                vf = pre[:, 1280:1536]
                for t in range(TILES):
                    mm(ps_s[:, 0:P], kf[:, P * t:P * t + P], vf[:, P * t:P * t + P], t == 0, t == TILES - 1)
                for t in range(TILES):
                    last = mm(ps_s[:, P:2 * P], kf[:, P * t:P * t + P], ones, t == 0, t == TILES - 1)
                last.then_inc(pre_pe, 1)
                dve("k_state")
                qf = pre[:, 768:1024]
                mm(ps_o[:, 0:TOKENS], lnt[:, 0, 0:P], qf, True, True)
                mm(ps_o[:, TOKENS:2 * TOKENS], lnt[:, 1, 0:P], qf, True, True).then_inc(pre_pe, 1)
                dve("mix")
                mm(ps_pt[:, 0:TOKENS], wpt, lnt[:, 5, :], True, True).then_inc(pre_pe, 1)
                act("out")

            def turn_qk(u, s):
                for i, ps, normed, read, done in ((0, ps_tq, q_normed, q_turned, tq_done),
                                                  (1, ps_tk, k_normed, k_turned, tk_done)):
                    pe.wait_ge(normed, u + 1)
                    wait(pe, read, u)
                    for c in range(PAIRS):
                        last = nc.tensor.transpose(ps[:, P * c:P * c + P], qk[:, s, i, P * c:P * c + P], ident[:])
                    last.then_inc(done, 1)

            def turn_p(u, s):
                pe.wait_ge(p_normed, u + 1)
                wait(pe, p_turned, u)
                for c in range(PAIRS):
                    last = nc.tensor.transpose(ps_pt[:, P * c:P * c + P], prob[:, s, P * c:P * c + P], ident[:])
                last.then_inc(pt_done, 1)

            def project(n, j):
                u = UNITS * n + j
                octet, tile = j // 2, j % 2
                if j == 0:
                    pe.wait_ge(xs_ready, n + 1)
                    pe.wait_ge(w_split, n // BATCHES * SLICES + SLICES)
                base = n // BATCHES % 2 * (3 * INNER)
                wait(pe, k_scaled, u)
                toks = slice(P * tile, P * tile + P)
                for i, ps, done in ((0, ps_q, q_done), (1, ps_k, k_done), (2, ps_v, v_done)):
                    if i == 2:
                        wait(pe, v_copied, u)
                        if j == 0 and live_batch(n - 2):
                            pe.wait_ge(var_ready, n - 1)
                        if j == 0 and live_batch(n - 3):
                            pe.wait_ge(x_ready, BATCHES + n - 2)
                        if j == 1 and live_batch(n - 2):
                            pe.wait_ge(ff1_copied, FF_N * (n - 2) + 2)
                        if j == 2 and live_batch(n - 2):
                            pe.wait_ge(ff1_copied, FF_N * (n - 2) + 3)
                        if j == 3 and live_batch(n - 1):
                            pe.wait_ge(centered, n)
                    cols = span(base + i * INNER + octet * OCTET, OCTET)
                    mm(ps[:], xs_hi[:, toks], w_hi[:, cols], True, False)
                    mm(ps[:], xs_hi[:, toks], w_lo[:, cols], False, False)
                    mm(ps[:], xs_lo[:, toks], w_hi[:, cols], False, True).then_inc(done, 1)

            def scores(u, j, s):
                octet, tile = j // 2, j % 2
                pe.wait_ge(q_turned, u + 1)
                pe.wait_ge(k_turned, u + 1)
                wait(pe, sub_done, u)
                mm(ps_s[:], ident_b[:], mask_b[:, tile, :], True, True)
                for odd in range(2):
                    for c in range(PAIRS):
                        for half in range(2):
                            w = 2 * half + odd
                            g = 2 * c + half
                            last = mm(ps_s[64 * odd:64 * odd + 64, 64 * g:64 * g + 64],
                                      q_bd[:, s, 4 * c + w].rearrange("p a b -> p (a b)"),
                                      k_t[:, octet, c, WINDOW * (4 * tile + w):WINDOW * (4 * tile + w) + 64],
                                      False, True, skip_group_check=True)
                last.then_inc(s_done, 1)

            def values(u, n, j, s):
                pe.wait_ge(p_turned, u + 1)
                pe.wait_ge(v_shifted[j], (n + 1) * (32 if j % 2 else 16))
                wait(pe, attn_copied, u)
                for head in range(2):
                    for c in range(PAIRS):
                        for odd in range(2):
                            v = v_own if odd else v_back
                            o = ps_o[64 * head:64 * head + 64, P * c:P * c + P].rearrange(
                                "p (h o q) -> p h o q", h=2, o=2)[:, :, odd, :]
                            last = mm(o, v[:, j, 64 * (2 * c + head):64 * (2 * c + head) + 64],
                                      p_bd[:, s, 4 * c + 2 * odd + head].rearrange("p a b -> p (a b)"), True, True,
                                      skip_group_check=True)
                last.then_inc(o_done, 1)

            def out_projection(m):
                if isinstance(m, int) and m > 0:
                    pe.wait_ge(ff1_copied, FF_N * m)
                pe.wait_ge(attn_copied, UNITS * m + UNITS)
                pe.wait_ge(wo_loaded, m // BATCHES * 16 + 16)
                for c in range(CHUNKS):
                    last = mm(ps_v[:, 0:TOKENS], wo_sb[:, c, :], attn_t[:, c, :], c == 0, c == CHUNKS - 1)
                last.then_inc(wo_done, 1)

            def ff_up(m, i):
                rows = FF_ROWS[i]
                if i == 0:
                    if isinstance(m, int):
                        pe.wait_ge(x_ready, BATCHES + m)
                    pe.wait_ge(xn_ready, m + 1)
                    pe.wait_ge(w1_loaded, m // BATCHES * 32 + 32)
                else:
                    pe.wait_ge(ff1_copied, FF_N * m + i)
                mm(ps_v[0:rows, 0:TOKENS], w1_sb[:, P * i:P * i + rows], xn[:], True, True)
                mm(ps_v[0:rows, TOKENS:2 * TOKENS], w1_sb[:, FF + P * i:FF + P * i + rows], xn[:], True, True
                   ).then_inc(ff1_done, 1)

            def ff_down(m):
                pe.wait_ge(ff_mixed, m + 1)
                pe.wait_ge(w2_loaded, m // BATCHES * 32 + 32)
                if live_batch(m + 1):
                    pe.wait_ge(var_ready, m + 2)
                for i, rows in enumerate(FF_ROWS):
                    last = mm(ps_v[:, 0:TOKENS], w2_sb[0:rows, i, :], ff_a[0:rows, i, :], i == 0, i == FF_N - 1)
                last.then_inc(ff2_done, 1)

            def body(n, _=True):
                for j in range(UNITS):
                    u = UNITS * n + j
                    if live(u):
                        project(n, j)
                    if live(u - 1):
                        turn_qk(u - 1, (j - 1) % 2)
                    if live(u - 2):
                        turn_p(u - 2, j % 2)
                    if live(u):
                        pe.wait_ge(v_copied, u + 1)
                    if j == 0 and live_batch(n - 2):
                        ff_up(n - 2, 0)
                    if j == 1 and live_batch(n - 2):
                        ff_up(n - 2, 2)
                    if j == 2 and live_batch(n - 1):
                        out_projection(n - 1)
                    if j == 3 and live_batch(n - 1):
                        pe.wait_ge(ln_squared, n)
                        mm(ps_v[:, 0:TOKENS], mean_w[:], lnt[:, 0, :], True, True).then_inc(var_done, 1)
                    if live(u - 1):
                        scores(u - 1, (j - 1) % UNITS, (j - 1) % 2)
                    if live(u - 2):
                        values(u - 2, n if j >= 2 else n - 1, (j - 2) % UNITS, j % 2)
                    if j == 0 and live_batch(n - 2):
                        ff_up(n - 2, 1)
                    if j == 2 and live_batch(n - 1):
                        pe.wait_ge(mid_done, 3 * n)
                        mm(ps_v[:, 0:TOKENS], mean_w[:], xs[:], True, True).then_inc(mean_done, 1)
                    if j == 3 and live_batch(n - 2):
                        ff_down(n - 2)

            iterations(pe, body)

        @block.scalar
        def _(act):
            nc.scalar.preload_act_table_set("natural_log_exp_and_others")
            with act.Fori(0, BATCHES) as b:
                def dve(step):
                    act.wait_ge(pre_dve, b * len(PRE_DVE) + PRE_DVE.index(step) + 1)

                def own(step):
                    act.wait_ge(pre_act, b * len(PRE_ACT) + PRE_ACT.index(step) + 1)

                dve("center")
                nc.scalar.activation(pre[:, 512:768], pre[:, 256:512], ACT.Square).then_inc(pre_act, 1)
                dve("var")
                nc.scalar.activation(lnt[:, 2, :], lnt[:, 3, :], ACT.Ln).then_inc(pre_act, 1)
                own("ln")
                nc.scalar.activation(lnt[:, 4, :], lnt[:, 2, :], ACT.Exp, scale=-0.5).then_inc(pre_act, 1)
                dve("q_neg")
                nc.scalar.activation(pre[:, 1536:1792], pre[:, 1536:1792], ACT.Exp).then_inc(pre_act, 1)
                dve("k_neg")
                nc.scalar.activation(pre[:, 1792:2048], pre[:, 1792:2048], ACT.Exp).then_inc(pre_act, 1)
                act.wait_ge(pre_pe, (b + 1) * len(PRE_PE))
                nc.scalar.activation(s_out[:, columns(b)], ps_pt[:, 0:TOKENS], ACT.Identity,
                                     bias=bp_sb).then_inc(pre_act, 1)

            def copy(o, i):
                return nc.scalar.copy(o, i)

            def body(n, _=True):
                for j in range(UNITS):
                    u = UNITS * n + j
                    s = j % 2
                    if j == 3 and live_batch(n - 1):
                        act.wait_ge(centered, n)
                        nc.scalar.activation(lnt[:, 0, :], xc[:], ACT.Square).then_inc(ln_squared, 1)
                    if live(u):
                        wait(act, ssq_done, u - 1)
                        act.wait_ge(q_done, u + 1)
                        nc.scalar.activation(squares[:, s, 0:OCTET], ps_q[:], ACT.Square).then_inc(q_squared, 1)
                        act.wait_ge(k_done, u + 1)
                        nc.scalar.activation(squares[:, s, OCTET:2 * OCTET], ps_k[:], ACT.Square).then_inc(k_squared, 1)
                        wait(act, o_done, u - 2)
                        act.wait_ge(v_done, u + 1)
                        copy(v_own[:, j, :], ps_v[:]).then_inc(v_copied, 1)
                    if live(u - 1):
                        s1, j1 = (j - 1) % 2, (j - 1) % UNITS
                        octet, tile = j1 // 2, j1 % 2
                        wait(act, s_done, u - 2)
                        act.wait_ge(tq_done, u)
                        for h in range(2):
                            rows = slice(64 * h, 64 * h + 64)
                            last = copy(q_bd[rows, s1, :, h, :],
                                        ps_tq[rows, :].rearrange("p (g q) -> p g q", q=WINDOW))
                        last.then_inc(q_turned, 1)
                        act.wait_ge(tk_done, u)
                        copy(k_t[:, octet, :, WINDOW + P * tile:WINDOW + P * tile + P],
                             ps_tk[:].rearrange("p (c t) -> p c t", t=P)).then_inc(k_turned, 1)
                    if live(u - 2):
                        wait(act, o_done, u - 3)
                        act.wait_ge(pt_done, u - 1)
                        for h in range(2):
                            rows = slice(64 * h, 64 * h + 64)
                            last = copy(p_bd[rows, s, :, h, :],
                                        ps_pt[rows, :].rearrange("p (g q) -> p g q", q=WINDOW))
                        last.then_inc(p_turned, 1)
                    if live(u):
                        act.wait_ge(ssq_clamped, u + 1)
                        nc.scalar.activation(ssq_ln[:, s, :], ssq_c[:, s, :], ACT.Ln).then_inc(ssq_logged, 1)
                        act.wait_ge(ssq_logged, u + 1)
                        nc.scalar.activation(rn_0[:, s, :], ssq_ln[:, s, :], ACT.Exp, scale=-0.5).then_inc(rn_started, 1)
                    def ff_copy(m, i):
                        rows = FF_ROWS[i]
                        act.wait_ge(ff1_done, FF_N * m + i + 1)
                        if i == 0:
                            wait(act, ff2_done, m)
                            act.wait_ge(w1_loaded, m // BATCHES * 32 + 32)
                        nc.scalar.activation(ff_a[0:rows, i, :], ps_v[0:rows, 0:TOKENS], ACT.Identity,
                                             bias=b1_sb[0:rows, i:i + 1])
                        nc.scalar.activation(ff_g[0:rows, i, :], ps_v[0:rows, TOKENS:2 * TOKENS], ACT.Identity,
                                             bias=b1_sb[0:rows, FF_N + i:FF_N + i + 1]).then_inc(ff1_copied, 1)

                    if j == 0 and live_batch(n - 2):
                        ff_copy(n - 2, 0)
                    if j == 1 and live_batch(n - 2):
                        ff_copy(n - 2, 2)
                    if j == 2 and live_batch(n - 2):
                        act.wait_ge(ff1_copied, FF_N * (n - 1))
                        nc.scalar.activation(ff_g[:].rearrange("p a b -> p (a b)"),
                                             ff_g[:].rearrange("p a b -> p (a b)"), ACT.Gelu).then_inc(gelu_done, 1)
                        nc.scalar.preload_act_table_set("natural_log_exp_and_others")
                    if j == 3 and live_batch(n - 1):
                        act.wait_ge(var_ready, n)
                        nc.scalar.activation(lnt[:, 2, :], lnt[:, 1, :], ACT.Ln).then_inc(ln_logged, 1)
                        act.wait_ge(ln_logged, n)
                        nc.scalar.activation(lnt[:, 3, :], lnt[:, 2, :], ACT.Exp, scale=-0.5).then_inc(ln_started, 1)
                    if live(u - 1):
                        act.wait_ge(sub_done, u)
                        nc.scalar.activation(prob[:, (j - 1) % 2, :], prob[:, (j - 1) % 2, :], ACT.Exp,
                                             scale=QK_SCALE).then_inc(exp_done, 1)
                    if live(u - 2):
                        j2 = (j - 2) % UNITS
                        octet, tile = j2 // 2, j2 % 2
                        m = n if j >= 2 else n - 1
                        wait(act, wo_done, m)
                        act.wait_ge(o_done, u - 1)
                        copy(attn_t[:, PAIRS * octet:PAIRS * octet + PAIRS, P * tile:P * tile + P],
                             ps_o[:].rearrange("p (c t) -> p c t", t=P)).then_inc(attn_copied, 1)
                    if j == 0 and live_batch(n - 2):
                        ff_copy(n - 2, 1)

            iterations(act, body)
            act.wait_ge(x_ready, BATCHES + STEPS)
            for b in range(BATCHES):
                nc.scalar.activation(squares[:].rearrange("p a b -> p (a b)")[:, columns(b)], x_run[:, columns(b)],
                                     ACT.Exp, scale=-1.0).then_inc(silu_exp, 1)

        @block.vector
        def _(dve):
            V = nc.vector
            V.memset(mean_w[:], 1.0 / P)
            V.memset(ones, 1.0)
            V.memset(xs_hi[64:P, 0:1].bitcast(F32), 0.0)
            V.memset(xs_lo[64:P, 0:1].bitcast(F32), 0.0)
            V.memset(xs[64:P, 0:1], 0.0).then_inc(pool_ready, 1)
            dve.wait_ge(consts_loaded, 16 * 13)
            V.tensor_copy(ident_b[:], ident[:])
            V.tensor_copy(mask_b[:].rearrange("p a b -> p (a b)"), mask_f).then_inc(consts_ready, 1)
            for l in range(DEPTH):
                for i in range(4):
                    sc = (qsc if i < 2 else ksc)[:, HEAD * l:HEAD * l + HEAD]
                    sc = sc.rearrange("p (a c) -> p a c", a=2)
                    if i % 2:
                        sc = sc[:, ::-1, :]
                    at = (4 * l + i) * TILES * HEAD
                    for t in range(TILES):
                        last = V.tensor_tensor(
                            table[:, at + HEAD * t:at + HEAD * t + HEAD].rearrange("p (a c) -> p a c", a=2),
                            rot_sb[:, (TILES * i + t) * HEAD:(TILES * i + t + 1) * HEAD].rearrange("p (a c) -> p a c", a=2),
                            sc, ALU.mult)
            last.then_inc(consts_ready, 1)

            def split_slice(k):
                raw = w_raw[:, span(k % 2 * SLICE, SLICE)]
                to = span(k % (2 * SLICES) * SLICE, SLICE)
                dve.wait_ge(raw_loaded, k * 16 + 16)
                V.tensor_copy(w_hi[:, to], raw).then_inc(w_rounded, 1)
                dve.wait_ge(w_rounded, k + 1)
                V.tensor_tensor(w_lo[:, to], raw, w_hi[:, to].bitcast(F32), ALU.subtract).then_inc(w_split, 1)

            for k in range(SLICES):
                split_slice(k)

            dve.wait_ge(x_loaded, 16 * BATCHES)
            with dve.Fori(0, BATCHES) as b:
                def step(name, ins):
                    ins.then_inc(pre_dve, 1)

                def own(name):
                    dve.wait_ge(pre_dve, b * len(PRE_DVE) + PRE_DVE.index(name) + 1)

                def pe(name):
                    dve.wait_ge(pre_pe, b * len(PRE_PE) + PRE_PE.index(name) + 1)

                def act(name):
                    dve.wait_ge(pre_act, b * len(PRE_ACT) + PRE_ACT.index(name) + 1)

                xn_b, xc_b = pre[:, 0:256], pre[:, 256:512]
                q_f, k_f, v_f = pre[:, 768:1024], pre[:, 1024:1280], pre[:, 1280:1536]
                q_e, k_e = pre[:, 1536:1792], pre[:, 1792:2048]
                kv = ps_tk[:].rearrange("p (t c) -> p t c", t=TILES)

                def tiled(t):
                    return t.rearrange("p (t c) -> p t c", t=TILES)

                var, r0 = lnt[:, 3, :], lnt[:, 4, :]
                pe("mean")
                step("center", V.tensor_tensor(xc_b, x_in[:, columns(b)], ps_q[:, 0:TOKENS], ALU.subtract))
                pe("var")
                step("var", V.tensor_scalar(var, ps_k[:, 0:TOKENS], LN_EPS, None, ALU.add))
                act("rsqrt")
                own("var")
                step("newton_a", V.scalar_tensor_tensor(out=lnt[:, 2, :], in0=var, scalar=-0.5, in1=r0,
                                                        op0=ALU.mult, op1=ALU.mult))
                own("newton_a")
                step("newton_b", V.tensor_tensor(lnt[:, 5, :], lnt[:, 2, :], r0, ALU.mult))
                own("newton_b")
                step("rstd", V.scalar_tensor_tensor(out=lnt[:, 2, :], in0=lnt[:, 5, :], scalar=1.5, in1=r0,
                                                    op0=ALU.add, op1=ALU.mult))
                own("rstd")
                step("xn", V.tensor_tensor(xn_b, xc_b, lnt[:, 2, :], ALU.mult))
                own("xn")
                step("keep", V.tensor_copy(x_run[:, columns(b)], xn_b))
                pe("qkv")
                step("q_neg", V.tensor_scalar(q_e, ps_tq[:, 0:TOKENS], 0.0, None, ALU.min))
                step("k_neg", V.tensor_scalar(tiled(k_e), kv[:, :, 0:P], 0.0, None, ALU.min))
                step("v_copy", V.tensor_copy(tiled(v_f), kv[:, :, P:2 * P]))
                mix = lnt[:, 2, :]
                step("conv_mid", V.tensor_scalar(mix, xn_b, conv_sb[:, 1:2], convb_sb, ALU.mult, ALU.add))
                own("conv_mid")
                step("conv_left", V.scalar_tensor_tensor(out=mix[:, 1:TOKENS], in0=xn_b[:, 0:TOKENS - 1],
                                                         scalar=conv_sb[:, 0:1], in1=mix[:, 1:TOKENS],
                                                         op0=ALU.mult, op1=ALU.add))
                own("conv_left")
                step("conv_right", V.scalar_tensor_tensor(out=mix[:, 0:TOKENS - 1], in0=xn_b[:, 1:TOKENS],
                                                          scalar=conv_sb[:, 2:3], in1=mix[:, 0:TOKENS - 1],
                                                          op0=ALU.mult, op1=ALU.add))
                act("q_exp")
                step("q_feat", V.scalar_tensor_tensor(out=q_f, in0=ps_tq[:, 0:TOKENS], scalar=0.0, in1=q_e,
                                                      op0=ALU.max, op1=ALU.add))
                act("k_exp")
                step("k_feat", V.scalar_tensor_tensor(out=tiled(k_f), in0=kv[:, :, 0:P], scalar=0.0, in1=tiled(k_e),
                                                      op0=ALU.max, op1=ALU.add))
                pe("state")
                step("kv_state", V.tensor_tensor(lnt[:, 0, 0:P], ps_s[:, 0:P], block_sb, ALU.mult))
                step("k_state", V.tensor_tensor(lnt[:, 1, 0:P], ps_s[:, P:2 * P], block_sb, ALU.mult))
                pe("read")
                step("den", V.tensor_scalar(lnt[:, 3, :], ps_o[:, TOKENS:2 * TOKENS], 1e-6, None, ALU.max))
                own("den")
                step("den_inv", V.reciprocal(lnt[:, 4, :], lnt[:, 3, :]))
                own("den_inv")
                step("attn", V.tensor_tensor(lnt[:, 3, :], ps_o[:, 0:TOKENS], lnt[:, 4, :], ALU.mult))
                own("attn")
                own("conv_right")
                step("mix", V.tensor_tensor(lnt[:, 5, :], lnt[:, 3, :], mix, ALU.add))
                dve.wait_ge(pre_act, (b + 1) * len(PRE_ACT))
            V.sem_inc(x_ready, BATCHES)

            def heads(t):
                return t.rearrange("p (h d) -> p h d", d=HEAD)

            def halves(t):
                return t.rearrange("p (h a c) -> p h a c", a=2, c=HEAD // 2)

            def round_x(n):
                dve.wait_ge(x_ready, n + 1)
                wait(dve, v_done, UNITS * n)
                b = n % BATCHES * TOKENS
                V.tensor_copy(xs_hi[0:64, :], x_run[0:64, span(b, TOKENS)])
                V.tensor_copy(xs_hi[64:P, 1:TOKENS], x_run[64:P, span(b, TOKENS - 1)]).then_inc(xs_rounded, 1)
                dve.wait_ge(xs_rounded, n + 1)
                V.tensor_tensor(xs_lo[0:64, :], x_run[0:64, span(b, TOKENS)], xs_hi[0:64, :].bitcast(F32), ALU.subtract)
                V.tensor_tensor(xs_lo[64:P, 1:TOKENS], x_run[64:P, span(b, TOKENS - 1)],
                                xs_hi[64:P, 1:TOKENS].bitcast(F32), ALU.subtract).then_inc(xs_ready, 1)

            def rotate(n, j):
                u = UNITS * n + j
                s = j % 2
                tile = j % 2
                wait(dve, tk_done, u - 1)
                for i, ps, read, scaled, added in ((0, ps_q, q_squared, q_scaled, q_added),
                                                   (1, ps_k, k_squared, k_scaled, k_added)):
                    wait(dve, added, u - 1)
                    dve.wait_ge(read, u + 1)
                    at = n // BATCHES * (4 * TILES * HEAD) + (2 * i * TILES + tile) * HEAD
                    cos = table[:, span(at, HEAD)]
                    sin = table[:, span(at + TILES * HEAD, HEAD)]
                    V.tensor_tensor(heads(qk[:, s, i, :]), heads(ps[:]),
                                    cos.unsqueeze(1).to_broadcast([P, 8, HEAD]), ALU.mult)
                    V.tensor_tensor(halves(qk_rot[:, s, i, :]), halves(ps[:])[:, :, ::-1, :],
                                    sin.rearrange("p (a c) -> p a c", a=2).unsqueeze(1).to_broadcast([P, 8, 2, HEAD // 2]),
                                    ALU.mult).then_inc(scaled, 1)

            def norms(u, s):
                V.tensor_reduce(ssq[:, s, :], squares[:, s, :].rearrange("p (h d) -> p h d", d=HEAD), AX,
                                ALU.add).then_inc(ssq_done, 1)
                dve.wait_ge(ssq_done, u + 1)
                V.tensor_scalar(ssq_c[:, s, :], ssq[:, s, :], 1e-24, SQ_SCALE, ALU.max, ALU.mult).then_inc(ssq_clamped, 1)

            def newton(u, s):
                dve.wait_ge(rn_started, u + 1)
                wait(dve, k_normed, u - 1)
                V.scalar_tensor_tensor(out=rn_a[:, s, :], in0=ssq_c[:, s, :], scalar=-0.5, in1=rn_0[:, s, :],
                                       op0=ALU.mult, op1=ALU.mult).then_inc(rn_step, 1)
                dve.wait_ge(rn_step, 2 * u + 1)
                V.tensor_tensor(rn_b[:, s, :], rn_a[:, s, :], rn_0[:, s, :], ALU.mult).then_inc(rn_step, 1)
                dve.wait_ge(rn_step, 2 * u + 2)
                V.scalar_tensor_tensor(out=rnorm[:, s, :], in0=rn_b[:, s, :], scalar=1.5, in1=rn_0[:, s, :],
                                       op0=ALU.add, op1=ALU.mult).then_inc(rnorm_done, 1)

            def less_max(u, s):
                dve.wait_ge(s_done, u + 1)
                V.tensor_reduce(row_max[:, s, :], heads(ps_s[:]), AX, ALU.max).then_inc(max_done, 1)
                dve.wait_ge(max_done, u + 1)
                wait(dve, pt_done, u - 1)
                V.tensor_tensor(heads(prob[:, s, :]), heads(ps_s[:]),
                                row_max[:, s, :].unsqueeze(2).to_broadcast([P, 8, HEAD]),
                                ALU.subtract).then_inc(sub_done, 1)

            def sums(u, s):
                dve.wait_ge(exp_done, u + 1)
                V.tensor_reduce(row_sum[:, s, :], heads(prob[:, s, :]), AX, ALU.add).then_inc(sum_done, 1)
                dve.wait_ge(sum_done, u + 1)
                wait(dve, p_normed, u - 1)
                V.reciprocal(row_inv[:, s, :], row_sum[:, s, :]).then_inc(inv_done, 1)

            def after_attention(m):
                dve.wait_ge(wo_done, m + 1)
                b = m % BATCHES * TOKENS
                V.tensor_tensor(x_mid[:, span(m % 2 * TOKENS, TOKENS)], x_run[:, span(b, TOKENS)], ps_v[:, 0:TOKENS], ALU.add).then_inc(mid_done, 1)
                V.tensor_tensor(xs[0:64, :], x_run[0:64, span(b, TOKENS)], ps_v[0:64, 0:TOKENS],
                                ALU.add).then_inc(mid_done, 1)
                V.tensor_tensor(xs[64:P, 1:TOKENS], x_run[64:P, span(b, TOKENS - 1)], ps_v[64:P, 0:TOKENS - 1],
                                ALU.add).then_inc(mid_done, 1)

            def ln_center(m):
                dve.wait_ge(mean_done, m + 1)
                dve.wait_ge(mid_done, 3 * m + 3)
                V.tensor_tensor(xc[:], xs[:], ps_v[:, 0:TOKENS], ALU.subtract).then_inc(centered, 1)

            def ln_var(m):
                dve.wait_ge(var_done, m + 1)
                V.tensor_scalar(lnt[:, 1, :], ps_v[:, 0:TOKENS], LN_EPS, None, ALU.add).then_inc(var_ready, 1)

            def ln_finish(m):
                dve.wait_ge(ln_started, m + 1)
                var, r0 = lnt[:, 1, :], lnt[:, 3, :]
                V.scalar_tensor_tensor(out=lnt[:, 4, :], in0=var, scalar=-0.5, in1=r0,
                                       op0=ALU.mult, op1=ALU.mult).then_inc(ln_step, 1)
                dve.wait_ge(ln_step, 4 * m + 1)
                V.tensor_tensor(lnt[:, 5, :], lnt[:, 4, :], r0, ALU.mult).then_inc(ln_step, 1)
                dve.wait_ge(ln_step, 4 * m + 2)
                V.scalar_tensor_tensor(out=lnt[:, 4, :], in0=lnt[:, 5, :], scalar=1.5, in1=r0,
                                       op0=ALU.add, op1=ALU.mult).then_inc(ln_step, 1)
                dve.wait_ge(ln_step, 4 * m + 3)
                V.tensor_tensor(lnt[:, 5, :], xc[:], lnt[:, 4, :], ALU.mult).then_inc(ln_step, 1)
                dve.wait_ge(ln_step, 4 * m + 4)
                wait(dve, ff1_done, FF_N * m)
                dve.wait_ge(ln_loaded, m // BATCHES * 32 + 32)
                V.tensor_scalar(xn[:], lnt[:, 5, :], ln_sb[:, 0:1], ln_sb[:, 1:2], ALU.mult, ALU.add).then_inc(xn_ready, 1)

            def ff_gate(m):
                dve.wait_ge(gelu_done, m + 1)
                V.tensor_tensor(ff_a[:], ff_a[:], ff_g[:], ALU.mult).then_inc(ff_mixed, 1)

            def after_ff(m):
                dve.wait_ge(ff2_done, m + 1)
                dve.wait_ge(w2_loaded, m // BATCHES * 32 + 32)
                V.scalar_tensor_tensor(out=x_run[:, columns(m)], in0=ps_v[:, 0:TOKENS], scalar=b2_sb[:, 0:1],
                                       in1=x_mid[:, span(m % 2 * TOKENS, TOKENS)], op0=ALU.add, op1=ALU.add).then_inc(x_ready, 1)

            def body(n, last_layer=False):
                split = n < (DEPTH - 1) * BATCHES if isinstance(n, int) else not last_layer
                for j in range(UNITS):
                    u = UNITS * n + j
                    if j == 3 and live_batch(n - 1):
                        ln_center(n - 1)
                    if live(u):
                        rotate(n, j)
                    if j == 3 and live(4 * (n + 1)):
                        round_x(n + 1)
                    if live(u):
                        norms(u, j % 2)
                    if j == 2 and live_batch(n - 1):
                        after_attention(n - 1)
                    if j == 3 and live_batch(n - 1):
                        ln_var(n - 1)
                    if live(u):
                        newton(u, j % 2)
                    if live(u - 1):
                        less_max(u - 1, (j - 1) % 2)
                    if j == 0 and split:
                        wait(dve, v_done, UNITS * n)
                        split_slice(n + SLICES)
                    if j == 3 and live_batch(n - 2):
                        ff_gate(n - 2)
                    if live(u - 1):
                        sums(u - 1, (j - 1) % 2)
                    if j == 3 and live_batch(n - 1):
                        ln_finish(n - 1)
                    if j == 3 and live_batch(n - 2):
                        after_ff(n - 2)

            round_x(0)
            dve.wait_ge(zeros_ready, 1)
            body(0)
            body(1)
            with dve.Fori(2, (DEPTH - 1) * BATCHES) as n:
                body(n)
            with dve.Fori((DEPTH - 1) * BATCHES, STEPS - 1) as n:
                body(n, True)
            body(STEPS - 1)
            body(STEPS)
            body(STEPS + 1)

            for b in range(BATCHES):
                c = columns(b)
                e = squares[:].rearrange("p a b -> p (a b)")[:, c]
                f = w_hi[:, c].bitcast(F32)
                dve.wait_ge(silu_exp, b + 1)
                fin = final_step
                V.tensor_scalar(e, e, 1.0, None, ALU.add).then_inc(fin, 1)
                dve.wait_ge(fin, 4 * b + 1)
                V.reciprocal(e, e).then_inc(fin, 1)
                dve.wait_ge(fin, 4 * b + 2)
                V.tensor_tensor(e, e, x_run[:, c], ALU.mult).then_inc(fin, 1)
                dve.wait_ge(fin, 4 * b + 3)
                V.tensor_tensor(e, e, s_out[:, c], ALU.mult).then_inc(fin, 1)
                dve.wait_ge(fin, 4 * b + 4)
                V.tensor_tensor(s_out[:, c], e, x_in[:, c], ALU.add).then_inc(final, 1)


def rotary_tables():
    f = np.float32
    half = np.arange(0, HEAD, 2, dtype=f)
    inv_freq = f(1.0) / np.power(f(10000.0), half / f(HEAD))
    t = np.arange(TOKENS, dtype=f)
    freqs = t[:, None] * inv_freq[None, :]
    base = (half + f(0.4 * HEAD)) / f(1.4 * HEAD)
    power = (t - f(TOKENS // 2)) / f(WINDOW // 2)
    scale = np.power(base[None, :], power[:, None])
    cos, sin = np.cos(freqs), np.sin(freqs)
    both = []
    for sc in (scale, f(1.0) / scale):
        both.append(np.concatenate([cos * sc, cos * sc], -1))
        both.append(np.concatenate([-sin * sc, sin * sc], -1))
    tab = np.stack(both) * f(SQ_SCALE ** 0.5)
    return np.ascontiguousarray(tab.reshape(4, TILES, P, HEAD).transpose(2, 0, 1, 3).reshape(P, -1).astype(f))


def score_masks():
    q = np.arange(WINDOW)[:, None]
    k = np.arange(WINDOW)[None, :]
    seen = np.concatenate([k >= q, k <= q], 1)
    m = np.where(seen, 0.0, MASKED)[None, None, :, None, None, None, :]
    m = np.broadcast_to(m, (2, 2, WINDOW, TILES, PAIRS, 2, 2 * WINDOW)).copy()
    m[0, :, :, 0, :, 0, 0:WINDOW] = MASKED
    return m.reshape(P, TILES * 512).astype(np.float32)


def kernel(**inputs):
    import concourse.bacc as bacc
    from concourse.bass_utils import run_bass_kernel_spmd

    a = {k.replace("L0_", ""): np.asarray(v) for k, v in inputs.items()}
    def turned(w):
        return np.ascontiguousarray(w.T)

    b1 = np.zeros((DEPTH, P, 2 * FF_N), np.float32)
    w2 = np.zeros((DEPTH, P, FF_N, DIM), np.float32)
    for i, rows in enumerate(FF_ROWS):
        b1[:, 0:rows, i] = a["ffn_b1"][:, P * i:P * i + rows]
        b1[:, 0:rows, FF_N + i] = a["ffn_b1"][:, FF + P * i:FF + P * i + rows]
        w2[:, 0:rows, i] = a["ffn_W2"][:, P * i:P * i + rows]
    arrays = {
        "x": turned(a["attn_x"].reshape(ALL, DIM)),
        "wq": turned(a["attn_Wq"]), "wk": turned(a["attn_Wk"]), "wv": turned(a["attn_Wv"]), "wp": turned(a["attn_Wp"]),
        "bp": a["attn_bp"].reshape(DIM, 1), "conv_w": a["attn_conv_w"], "conv_b": a["attn_conv_b"].reshape(DIM, 1),
        "wqkv": a["ffn_Wqkv"].reshape(DEPTH, DIM, SLICES, SLICE).transpose(0, 2, 1, 3).reshape(DEPTH * SLICES, DIM, SLICE),
        "q_scale": a["ffn_q_scale"].reshape(-1), "k_scale": a["ffn_k_scale"].reshape(-1),
        "wo": a["ffn_Wo"].reshape(DEPTH, CHUNKS, P, DIM).transpose(0, 2, 1, 3).reshape(DEPTH, P, CHUNKS * DIM),
        "ln_g": a["ffn_ln_g"].reshape(DEPTH, DIM, 1), "ln_b": a["ffn_ln_b"].reshape(DEPTH, DIM, 1),
        "w1": a["ffn_W1"], "b1": b1, "w2": w2.reshape(DEPTH, P, FF_N * DIM), "b2": a["ffn_b2"].reshape(DEPTH, DIM, 1),
        "rotary": rotary_tables(), "masks": score_masks(), "eye": np.eye(P, dtype=np.float32),
        "head_block": np.kron(np.eye(HEADS), np.ones((LINEAR_HEAD, LINEAR_HEAD))).astype(np.float32),
    }
    arrays = {k: np.ascontiguousarray(v) for k, v in arrays.items()}
    nc = bacc.Bacc("TRN2", target_bir_lowering=False, num_devices=1)
    aps = [nc.dram_tensor("in_" + k, v.shape, mybir.dt.from_np(v.dtype), kind="ExternalInput").ap()
           for k, v in arrays.items()]
    out = nc.dram_tensor("out", (P, ALL), F32, kind="ExternalOutput").ap()
    build(nc, *aps, out)
    r = run_bass_kernel_spmd(nc, [{"in_" + k: v for k, v in arrays.items()}], core_ids=[0])
    y = np.asarray(r.results[0]["out"])
    return np.ascontiguousarray(y.T).reshape(BATCHES, TOKENS, DIM)
```

```python
from contextlib import ExitStack

import numpy as np

import concourse.bass as bass
from concourse import mybir

F32 = mybir.dt.float32
F32R = mybir.dt.float32r
BF16 = mybir.dt.bfloat16
ALU = mybir.AluOpType
ACT = mybir.ActivationFunctionType
AX = mybir.AxisListType.X

P = 128
BATCHES, TOKENS, DIM = 8, 256, 128
DEPTH, HEADS, HEAD, WINDOW = 6, 16, 64, 32
INNER = HEADS * HEAD
FF = DIM * 4 * 2 // 3
QK_SCALE = 8.0
ALL = BATCHES * TOKENS
TILES = TOKENS // P
OCTET = 8 * HEAD
PAIRS = OCTET // P
CHUNKS = INNER // P
UNITS = 4
STEPS = DEPTH * BATCHES
LAG = 3
SLICES = 8
SLICE = 3 * INNER // SLICES
FF_ROWS = [min(P, FF - P * i) for i in range((FF + P - 1) // P)]
FF_N = len(FF_ROWS)
MASKED = -1.0e30
SQ_SCALE = 2.0 ** 16
LN_EPS = 1e-5
LINEAR_HEAD = DIM // HEADS

PRE_DVE = ["center", "var", "newton_a", "newton_b", "rstd", "xn", "keep", "q_neg", "k_neg", "v_copy",
           "conv_mid", "conv_left", "conv_right", "q_feat", "k_feat", "kv_state", "k_state", "den",
           "den_inv", "attn", "mix"]
PRE_ACT = ["square", "ln", "rsqrt", "q_exp", "k_exp", "out"]
PRE_PE = ["mean", "var", "qkv", "state", "read", "out"]


def build(nc, x, wq, wk, wv, wp, bp, conv_w, conv_b, wqkv, q_scale, k_scale, wo, ln_g, ln_b, w1, b1, w2, b2,
          rotary, masks, eye, head_block, out):
    with ExitStack() as ctx:
        def sb(name, shape, dt=F32):
            return ctx.enter_context(nc.sbuf_tensor(name, shape, dt))

        def bank(name):
            return ctx.enter_context(nc.psum_tensor(name, [P, 512], F32))

        def sem(name):
            return ctx.enter_context(nc.semaphore(name))

        x_in = sb("x_in", [P, ALL])
        x_run = sb("x_run", [P, ALL])
        s_out = sb("s_out", [P, ALL])
        w_hi = sb("w_hi", [P, 2 * 3 * INNER], F32R)
        w_lo = sb("w_lo", [P, 2 * 3 * INNER], F32R)
        w_raw = sb("w_raw", [P, 2 * SLICE])
        wo_sb = sb("wo_sb", [P, CHUNKS, DIM])
        w1_sb = sb("w1_sb", [P, 2 * FF])
        w2_sb = sb("w2_sb", [P, FF_N, DIM])
        b1_sb = sb("b1_sb", [P, 2 * FF_N])
        b2_sb = sb("b2_sb", [P, 1])
        ln_sb = sb("ln_sb", [P, 2])
        table = sb("table", [P, DEPTH * 4 * TILES * HEAD])
        ident = sb("ident", [P, P])
        ident_b = sb("ident_b", [P, P], BF16)
        mask_b = sb("mask_b", [P, TILES, 512], BF16)
        mean_w = sb("mean_w", [P, P])
        xs_hi = sb("xs_hi", [P, TOKENS], F32R)
        xs_lo = sb("xs_lo", [P, TOKENS], F32R)
        squares = sb("squares", [P, 2, 2 * OCTET])
        ssq = sb("ssq", [P, 2, 16])
        ssq_c = sb("ssq_c", [P, 2, 16])
        ssq_ln = sb("ssq_ln", [P, 2, 16])
        rn_0 = sb("rn_0", [P, 2, 16])
        rn_a = sb("rn_a", [P, 2, 16])
        rn_b = sb("rn_b", [P, 2, 16])
        rnorm = sb("rnorm", [P, 2, 16])
        qk = sb("qk", [P, 2, 2, OCTET])
        qk_rot = sb("qk_rot", [P, 2, 2, OCTET])
        q_bd = sb("q_bd", [P, 2, PAIRS * 4, 2, WINDOW])
        k_t = sb("k_t", [P, 2, PAIRS, WINDOW + TOKENS])
        prob = sb("prob", [P, 2, OCTET])
        p_bd = sb("p_bd", [P, 2, PAIRS * 4, 2, WINDOW])
        row_max = sb("row_max", [P, 2, 8])
        row_sum = sb("row_sum", [P, 2, 8])
        row_inv = sb("row_inv", [P, 2, 8])
        v_own = sb("v_own", [P, UNITS, OCTET])
        v_back = sb("v_back", [P, UNITS, OCTET])
        attn_t = sb("attn_t", [P, CHUNKS, TOKENS])
        x_mid = sb("x_mid", [P, 2 * TOKENS])
        xs = sb("xs", [P, TOKENS])
        xc = sb("xc", [P, TOKENS])
        lnt = sb("lnt", [P, 6, TOKENS])
        xn = sb("xn", [P, TOKENS])
        ff_a = sb("ff_a", [P, FF_N, TOKENS])
        ff_g = sb("ff_g", [P, FF_N, TOKENS])

        pre = qk_rot[:].rearrange("p a b c -> p (a b c)")
        wqt, wkvt, wpt = attn_t[:, 0, 0:P], attn_t[:, 1, :], attn_t[:, 2, 0:P]
        bp_sb, conv_sb, convb_sb = attn_t[:, 3, 0:1], attn_t[:, 3, 1:4], attn_t[:, 3, 4:5]
        block_sb = attn_t[:, 4, 0:P]
        ones = attn_t[:, 5, 0:P]
        qsc = attn_t[:, 6:8, :].rearrange("p a b -> p (a b)")
        ksc = prob[:, 0, 0:DEPTH * HEAD]
        rot_sb = squares[:, 0, 0:4 * TILES * HEAD]
        mask_f = qk[:, 0].rearrange("p a b -> p (a b)")

        ps_q, ps_k, ps_v, ps_qs, ps_tk, ps_po, ps_a, ps_f = (
            bank(n) for n in ("ps_q", "ps_k", "ps_v", "ps_qs", "ps_tk", "ps_po", "ps_a", "ps_f"))

        x_loaded, consts_loaded, raw_loaded, out_stored = sem("x_loaded"), sem("consts_loaded"), sem("raw_loaded"), sem("out_stored")
        wo_loaded, w1_loaded, w2_loaded, ln_loaded = (sem("wo_loaded_0"), sem("wo_loaded_1")), sem("w1_loaded"), sem("w2_loaded"), sem("ln_loaded")
        v_shifted = [sem(f"v_shifted_{j}") for j in range(UNITS)]
        memset_done, zeros_ready = sem("memset_done"), sem("zeros_ready")
        consts_ready, table_ready, w_split, w_rounded = sem("consts_ready"), sem("table_ready"), sem("w_split"), sem("w_rounded")
        pre_pe, pre_act, pre_dve = sem("pre_pe"), sem("pre_act"), sem("pre_dve")
        pool_passed = sem("pool_passed")
        x_ready, xs_rounded, xs_ready = sem("x_ready"), sem("xs_rounded"), sem("xs_ready")
        q_done, k_done, v_done = sem("q_done"), sem("k_done"), sem("v_done")
        tq_done, tk_done, pt_done, s_done, o_done = sem("tq_done"), sem("tk_done"), sem("pt_done"), sem("s_done"), sem("o_done")
        wo_half_done, wo_done, mean_done, var_done, ff1_done, ff2_done = sem("wo_half_done"), sem("wo_done"), sem("mean_done"), sem("var_done"), sem("ff1_done"), sem("ff2_done")
        q_squared, k_squared, v_copied, q_turned, k_turned, p_turned, exp_done, attn_copied = (
            sem(n) for n in ("q_squared", "k_squared", "v_copied", "q_turned", "k_turned", "p_turned", "exp_done", "attn_copied"))
        ssq_logged, rn_started, ln_squared, ln_logged, ln_started, ff1_copied, gelu_done, silu_exp = (
            sem(n) for n in ("ssq_logged", "rn_started", "ln_squared", "ln_logged", "ln_started", "ff1_copied", "gelu_done", "silu_exp"))
        q_scaled, k_scaled, ssq_done, ssq_clamped, rn_step, rnorm_done = (
            sem(n) for n in ("q_scaled", "k_scaled", "ssq_done", "ssq_clamped", "rn_step", "rnorm_done"))
        max_done, sub_done, sum_done, inv_done = sem("max_done"), sem("sub_done"), sem("sum_done"), sem("inv_done")
        xs_shifted, mid_done, centered, var_ready, ln_step, xn_ready, ff_mixed, final, final_step = (
            sem(n) for n in ("xs_shifted", "mid_done", "centered", "var_ready", "ln_step", "xn_ready", "ff_mixed", "final", "final_step"))
        q_added, k_added, q_normed, k_normed, p_normed = (
            sem(n) for n in ("q_added", "k_added", "q_normed", "k_normed", "p_normed"))

        CONSTS = 16 * 16

        def live(u):
            return not isinstance(u, int) or 0 <= u < UNITS * STEPS

        def live_batch(m):
            return not isinstance(m, int) or 0 <= m < STEPS

        def wait(eng, s, value):
            if not isinstance(value, int) or value > 0:
                eng.wait_ge(s, value)

        def columns(m):
            if isinstance(m, int):
                return slice(m % BATCHES * TOKENS, m % BATCHES * TOKENS + TOKENS)
            return bass.ds(m % BATCHES * TOKENS, TOKENS)

        def span(start, size):
            return slice(start, start + size) if isinstance(start, int) else bass.ds(start, size)

        def iterations(eng, body, last_layer_differs=False):
            for n in range(LAG):
                body(n)
            if last_layer_differs:
                with eng.Fori(LAG, (DEPTH - 1) * BATCHES) as n:
                    body(n)
                with eng.Fori((DEPTH - 1) * BATCHES, STEPS - 1) as n:
                    body(n, True)
                body(STEPS - 1)
            else:
                with eng.Fori(LAG, STEPS) as n:
                    body(n)
            for n in range(STEPS, STEPS + LAG):
                body(n)

        silu_e = squares[:].rearrange("p a b -> p (a b)")

        def silu_at(n, j):
            if not isinstance(n, int) or n < STEPS:
                return []
            slot = UNITS * (n - STEPS) + j
            if 1 <= slot < BATCHES:
                return [slot - 1]
            return [BATCHES - 1] if slot == UNITS * (LAG - 1) + 2 else []

        block = ctx.enter_context(nc.Block())

        @block.sync
        def _(sp):
            for b in range(BATCHES):
                sp.dma_start(x_in[:, columns(b)], x[:, columns(b)]).then_inc(x_loaded, 16)
            for dst, src in ((rot_sb, rotary), (qsc[:, 0:DEPTH * HEAD], q_scale.partition_broadcast(P)),
                             (ksc, k_scale.partition_broadcast(P)), (wqt, wq), (wkvt[:, 0:P], wk),
                             (wkvt[:, P:2 * P], wv), (wpt, wp), (bp_sb, bp), (conv_sb, conv_w), (convb_sb, conv_b),
                             (block_sb, head_block), (ident[:], eye), (mask_f, masks)):
                sp.dma_start(dst, src).then_inc(consts_loaded, 16)

            def load_slice(k):
                half = k % 2 * SLICE
                if isinstance(k, int):
                    wait(sp, raw_loaded, 16 * k)
                    wait(sp, w_split, k - 1)
                else:
                    sp.wait_ge(w_split, k)
                sp.dma_start(w_raw[:, span(half, SLICE)],
                             wqkv[k] if isinstance(k, int) else wqkv[bass.ds(k, 1)].rearrange("a p c -> (a p) c")
                             ).then_inc(raw_loaded, 16)

            def layer_of(t, l):
                return t[l] if isinstance(l, int) else t[bass.ds(l, 1)].rearrange("a p c -> (a p) c")

            def load_wo(l, h):
                wait(sp, (wo_half_done, wo_done)[h], BATCHES * l)
                cols = slice(h * CHUNKS // 2 * DIM, (h + 1) * CHUNKS // 2 * DIM)
                sp.dma_start(wo_sb[:].rearrange("p c d -> p (c d)")[:, cols],
                             (wo[l] if isinstance(l, int) else layer_of(wo, l))[:, cols]).then_inc(wo_loaded[h], 16)

            def load_ln(l):
                wait(sp, xn_ready, BATCHES * l)
                sp.dma_start(ln_sb[:, 0:1], layer_of(ln_g, l)).then_inc(ln_loaded, 16)
                sp.dma_start(ln_sb[:, 1:2], layer_of(ln_b, l)).then_inc(ln_loaded, 16)

            def load_w1(l):
                wait(sp, ff1_copied, FF_N * BATCHES * l)
                sp.dma_start(w1_sb[:], layer_of(w1, l)).then_inc(w1_loaded, 16)
                sp.dma_start(b1_sb[:], layer_of(b1, l)).then_inc(w1_loaded, 16)

            def load_w2(l):
                if not isinstance(l, int) or l > 0:
                    sp.wait_ge(x_ready, BATCHES + BATCHES * l)
                sp.dma_start(w2_sb[:].rearrange("p c d -> p (c d)"), layer_of(w2, l)).then_inc(w2_loaded, 16)
                sp.dma_start(b2_sb[:], layer_of(b2, l)).then_inc(w2_loaded, 16)

            def shift_v(n, j):
                wait(sp, v_copied, UNITS * n + j + 1)
                sp.dma_start(v_back[WINDOW:P, j, :], v_own[0:P - WINDOW, j, :]).then_inc(v_shifted[j], 16)
                if j % 2:
                    sp.dma_start(v_back[0:WINDOW, j, :], v_own[P - WINDOW:P, j - 1, :]).then_inc(v_shifted[j], 16)

            for k in range(2):
                load_slice(k)
            load_wo(0, 0)
            load_wo(0, 1)
            for load in (load_ln, load_w1, load_w2):
                load(0)
            for k in range(2, SLICES):
                load_slice(k)

            def body(n, b=3, l=0, slices=True):
                if slices:
                    load_slice(n + SLICES)
                for j in range(UNITS):
                    shift_v(n, j)
                    if b == 0 and j >= 2:
                        load_wo(l, j - 2)
                    if b == 1 and j == 3:
                        load_ln(l)
                    if b == 2 and j == 0:
                        load_w1(l)
                    if b == 2 and j == 2:
                        load_w2(l)

            body(0)
            body(1)
            with sp.Fori(2, BATCHES) as n:
                body(n)
            with sp.Fori(1, DEPTH - 1) as l:
                body(l * BATCHES, 0, l)
                body(l * BATCHES + 1, 1, l)
                body(l * BATCHES + 2, 2, l)
                with sp.Fori(3, BATCHES) as b:
                    body(l * BATCHES + b)
            n = (DEPTH - 1) * BATCHES
            body(n, 0, DEPTH - 1, slices=False)
            body(n + 1, 1, DEPTH - 1, slices=False)
            body(n + 2, 2, DEPTH - 1, slices=False)
            with sp.Fori(n + 3, STEPS) as n:
                body(n, slices=False)
            for b in range(BATCHES):
                wait(sp, final, b + 1)
                sp.dma_start(out[:, columns(b)], s_out[:, columns(b)]).then_inc(out_stored, 16)
            sp.wait_ge(out_stored, 16 * BATCHES)

        @block.gpsimd
        def _(pool):
            nc.gpsimd.memset(q_bd[:], 0.0)
            nc.gpsimd.memset(p_bd[:], 0.0)
            nc.gpsimd.memset(k_t[:, :, :, 0:WINDOW], 0.0)
            nc.gpsimd.memset(v_back[0:WINDOW, 0:UNITS:2, :], 0.0)
            nc.gpsimd.memset(ff_a[:], 0.0)
            nc.gpsimd.memset(ff_g[:], 0.0).then_inc(zeros_ready, 1)

            pool.wait_ge(consts_loaded, 16 * 13)
            for l in range(DEPTH):
                for i in range(4):
                    sc = (qsc if i < 2 else ksc)[:, HEAD * l:HEAD * l + HEAD]
                    sc = sc.rearrange("p (a c) -> p a c", a=2)
                    if i % 2:
                        sc = sc[:, ::-1, :]
                    at = (4 * l + i) * TILES * HEAD
                    for t in range(TILES):
                        last = nc.gpsimd.tensor_tensor(
                            table[:, at + HEAD * t:at + HEAD * t + HEAD].rearrange("p (a c) -> p a c", a=2),
                            rot_sb[:, (TILES * i + t) * HEAD:(TILES * i + t + 1) * HEAD].rearrange("p (a c) -> p a c", a=2),
                            sc, ALU.mult)
            last.then_inc(table_ready, 1)

            def passed():
                nc.gpsimd.sem_inc(pool_passed, 1)

            def split_slice(k):
                raw = w_raw[:, span(k % 2 * SLICE, SLICE)]
                to = span(k % (2 * SLICES) * SLICE, SLICE)
                pool.wait_ge(raw_loaded, k * 16 + 16)
                passed()
                nc.gpsimd.tensor_copy(w_hi[:, to], raw).then_inc(w_rounded, 1)
                pool.wait_ge(w_rounded, k + 1)
                passed()
                nc.gpsimd.tensor_tensor(w_lo[:, to], raw, w_hi[:, to].bitcast(F32), ALU.subtract).then_inc(w_split, 1)

            for k in range(SLICES):
                split_slice(k)

            def heads(t):
                return t.rearrange("p (h d) -> p h d", d=HEAD)

            def add_halves(u, s):
                for i, scaled, added in ((0, q_scaled, q_added), (1, k_scaled, k_added)):
                    pool.wait_ge(scaled, u + 1)
                    nc.gpsimd.tensor_tensor(qk[:, s, i, :], qk[:, s, i, :], qk_rot[:, s, i, :],
                                            ALU.add).then_inc(added, 1)

            def normalise(u, s):
                pool.wait_ge(rnorm_done, u + 1)
                for i, added, normed in ((0, q_added, q_normed), (1, k_added, k_normed)):
                    pool.wait_ge(added, u + 1)
                    nc.gpsimd.tensor_tensor(heads(qk[:, s, i, :]), heads(qk[:, s, i, :]),
                                            rnorm[:, s, 8 * i:8 * i + 8].unsqueeze(2).to_broadcast([P, 8, HEAD]),
                                            ALU.mult).then_inc(normed, 1)

            def divide(u, s):
                pool.wait_ge(inv_done, u + 1)
                nc.gpsimd.tensor_tensor(heads(prob[:, s, :]), heads(prob[:, s, :]),
                                        row_inv[:, s, :].unsqueeze(2).to_broadcast([P, 8, HEAD]),
                                        ALU.mult).then_inc(p_normed, 1)

            def ff_gate(m):
                pool.wait_ge(gelu_done, m + 1)
                nc.gpsimd.tensor_tensor(ff_a[:], ff_a[:], ff_g[:], ALU.mult).then_inc(ff_mixed, 1)

            def body(n, last_layer=False):
                split = n < (DEPTH - 1) * BATCHES if isinstance(n, int) else not last_layer
                for j in range(UNITS):
                    u = UNITS * n + j
                    if live(u - 2):
                        divide(u - 2, j % 2)
                    if live(u):
                        add_halves(u, j % 2)
                    if j == 1 and live_batch(n - 3):
                        ff_gate(n - 3)
                    if j == 2 and split:
                        wait(pool, v_done, UNITS * n)
                        split_slice(n + SLICES)
                    if live(u):
                        normalise(u, j % 2)

            iterations(pool, body, last_layer_differs=True)

        @block.tensor
        def _(pe):
            def mm(o, lhs, rhs, start, stop, **kw):
                return nc.tensor.matmul(o, lhs, rhs, start=start, stop=stop, **kw)

            pe.wait_ge(x_loaded, 16 * BATCHES)
            pe.wait_ge(consts_ready, 1)
            pe.wait_ge(memset_done, 1)

            with pe.Fori(0, BATCHES) as b:
                def dve(step):
                    pe.wait_ge(pre_dve, b * len(PRE_DVE) + PRE_DVE.index(step) + 1)

                def act(step, ago=0):
                    pe.wait_ge(pre_act, b * len(PRE_ACT) + PRE_ACT.index(step) + 1)

                xn_b = pre[:, 0:TOKENS]
                mm(ps_q[:, 0:TOKENS], mean_w[:], x_in[:, columns(b)], True, True).then_inc(pre_pe, 1)
                act("square")
                mm(ps_k[:, 0:TOKENS], mean_w[:], pre[:, 512:768], True, True).then_inc(pre_pe, 1)
                dve("xn")
                mm(ps_qs[:, 0:TOKENS], wqt, xn_b, True, True)
                for t in range(TILES):
                    last = mm(ps_tk[:, 256 * t:256 * t + 256], pre[:, P * t:P * t + P], wkvt, True, True)
                last.then_inc(pre_pe, 1)
                dve("k_feat")
                kf = pre[:, 1024:1280]
                vf = pre[:, 1280:1536]
                for t in range(TILES):
                    mm(ps_v[:, 0:P], kf[:, P * t:P * t + P], vf[:, P * t:P * t + P], t == 0, t == TILES - 1)
                for t in range(TILES):
                    last = mm(ps_v[:, P:2 * P], kf[:, P * t:P * t + P], ones, t == 0, t == TILES - 1)
                last.then_inc(pre_pe, 1)
                dve("k_state")
                qf = pre[:, 768:1024]
                mm(ps_a[:, 0:TOKENS], lnt[:, 0, 0:P], qf, True, True)
                mm(ps_a[:, TOKENS:2 * TOKENS], lnt[:, 1, 0:P], qf, True, True).then_inc(pre_pe, 1)
                dve("mix")
                mm(ps_f[:, 0:TOKENS], wpt, lnt[:, 5, :], True, True).then_inc(pre_pe, 1)
                act("out")

            def turn_qk(u, i, s):
                ps, normed, read, done = ((ps_qs, q_normed, sub_done, tq_done), (ps_tk, k_normed, k_turned, tk_done))[i]
                wait(pe, read, u)
                pe.wait_ge(normed, u + 1)
                for c in range(PAIRS):
                    last = nc.tensor.transpose(ps[:, P * c:P * c + P], qk[:, s, i, P * c:P * c + P], ident[:])
                last.then_inc(done, 1)

            def turn_p(u, s):
                wait(pe, attn_copied, u)
                pe.wait_ge(p_normed, u + 1)
                for c in range(PAIRS):
                    last = nc.tensor.transpose(ps_po[:, P * c:P * c + P], prob[:, s, P * c:P * c + P], ident[:])
                last.then_inc(pt_done, 1)

            def project(n, j, i, ps, free, done):
                u = UNITS * n + j
                octet, tile = j // 2, j % 2
                if j == 0 and i == 0:
                    pe.wait_ge(xs_ready, n + 1)
                    pe.wait_ge(w_split, n // BATCHES * SLICES + SLICES)
                wait(pe, free, u)
                toks = slice(P * tile, P * tile + P)
                cols = span(n // BATCHES % 2 * (3 * INNER) + i * INNER + octet * OCTET, OCTET)
                mm(ps[:], xs_hi[:, toks], w_hi[:, cols], True, False)
                mm(ps[:], xs_hi[:, toks], w_lo[:, cols], False, False)
                mm(ps[:], xs_lo[:, toks], w_hi[:, cols], False, True).then_inc(done, 1)

            def scores(u, j, s):
                octet, tile = j // 2, j % 2
                pe.wait_ge(q_turned, u + 1)
                pe.wait_ge(k_turned, u + 1)
                mm(ps_qs[:], ident_b[:], mask_b[:, tile, :], True, True)
                for odd in range(2):
                    for c in range(PAIRS):
                        for half in range(2):
                            w = 2 * half + odd
                            g = 2 * c + half
                            last = mm(ps_qs[64 * odd:64 * odd + 64, 64 * g:64 * g + 64],
                                      q_bd[:, s, 4 * c + w].rearrange("p a b -> p (a b)"),
                                      k_t[:, octet, c, WINDOW * (4 * tile + w):WINDOW * (4 * tile + w) + 64],
                                      False, True, skip_group_check=True)
                last.then_inc(s_done, 1)

            def values(u, n, j, s):
                pe.wait_ge(p_turned, u + 1)
                pe.wait_ge(v_shifted[j], (n + 1) * (32 if j % 2 else 16))
                for head in range(2):
                    for c in range(PAIRS):
                        for odd in range(2):
                            v = v_own if odd else v_back
                            o = ps_po[64 * head:64 * head + 64, P * c:P * c + P].rearrange(
                                "p (h o q) -> p h o q", h=2, o=2)[:, :, odd, :]
                            last = mm(o, v[:, j, 64 * (2 * c + head):64 * (2 * c + head) + 64],
                                      p_bd[:, s, 4 * c + 2 * odd + head].rearrange("p a b -> p (a b)"), True, True,
                                      skip_group_check=True)
                last.then_inc(o_done, 1)

            def out_projection(m, h):
                if h == 0:
                    wait(pe, mid_done, m)
                pe.wait_ge(attn_copied, UNITS * m + 2 * h + 2)
                pe.wait_ge(wo_loaded[h], m // BATCHES * 16 + 16)
                for c in range(CHUNKS // 2):
                    c += h * CHUNKS // 2
                    last = mm(ps_a[:, 0:TOKENS], wo_sb[:, c, :], attn_t[:, c, :], c == 0, c == CHUNKS - 1)
                last.then_inc((wo_half_done, wo_done)[h], 1)

            def ln_mean(m):
                pe.wait_ge(xs_shifted, 2 * m + 2)
                mm(ps_a[:, TOKENS:2 * TOKENS], mean_w[:], xs[:], True, True).then_inc(mean_done, 1)

            def ln_variance(m):
                pe.wait_ge(ln_squared, m + 1)
                wait(pe, ff1_copied, FF_N * m)
                mm(ps_f[:, 0:TOKENS], mean_w[:], lnt[:, 0, :], True, True).then_inc(var_done, 1)

            def ff_up(m, i):
                rows = FF_ROWS[i]
                if i == 0:
                    wait(pe, x_ready, BATCHES + m)
                    pe.wait_ge(xn_ready, m + 1)
                    pe.wait_ge(w1_loaded, m // BATCHES * 32 + 32)
                else:
                    pe.wait_ge(ff1_copied, FF_N * m + i)
                mm(ps_f[0:rows, 0:TOKENS], w1_sb[:, P * i:P * i + rows], xn[:], True, True)
                mm(ps_f[0:rows, TOKENS:2 * TOKENS], w1_sb[:, FF + P * i:FF + P * i + rows], xn[:], True, True
                   ).then_inc(ff1_done, 1)

            def ff_down(m):
                if live_batch(m + 1):
                    pe.wait_ge(var_ready, m + 2)
                pe.wait_ge(ff_mixed, m + 1)
                pe.wait_ge(w2_loaded, m // BATCHES * 32 + 32)
                for i, rows in enumerate(FF_ROWS):
                    last = mm(ps_f[:, 0:TOKENS], w2_sb[0:rows, i, :], ff_a[0:rows, i, :], i == 0, i == FF_N - 1)
                last.then_inc(ff2_done, 1)

            def body(n):
                for j in range(UNITS):
                    u = UNITS * n + j
                    for i, ps, free, done in ((0, ps_q, q_squared, q_done), (1, ps_k, k_squared, k_done)):
                        if live(u):
                            project(n, j, i, ps, free, done)
                        if i == 0 and j == 0 and live_batch(n - 2):
                            ln_mean(n - 2)
                        if i == 0 and j == 1 and live_batch(n - 2):
                            ln_variance(n - 2)
                        if i == 0 and j == 2 and live_batch(n - 3):
                            ff_down(n - 3)
                        if i == 0 and j == 3 and live_batch(n - 2):
                            ff_up(n - 2, 1)
                        if live(u - 1):
                            turn_qk(u - 1, i, (j - 1) % 2)
                    if live(u):
                        project(n, j, 2, ps_v, v_copied, v_done)
                    if live(u - 2):
                        turn_p(u - 2, j % 2)
                    if j == 1 and live_batch(n - 1):
                        out_projection(n - 1, 0)
                    if live(u - 1):
                        scores(u - 1, (j - 1) % UNITS, (j - 1) % 2)
                    if j == 0 and live_batch(n - 3):
                        ff_up(n - 3, 2)
                    if j == 2 and live_batch(n - 2):
                        ff_up(n - 2, 0)
                    if j == 3 and live_batch(n - 1):
                        out_projection(n - 1, 1)
                    if live(u - 2):
                        values(u - 2, n if j >= 2 else n - 1, (j - 2) % UNITS, j % 2)

            iterations(pe, body)

        @block.scalar
        def _(act):
            nc.scalar.preload_act_table_set("natural_log_exp_and_others")
            with act.Fori(0, BATCHES) as b:
                def dve(step):
                    act.wait_ge(pre_dve, b * len(PRE_DVE) + PRE_DVE.index(step) + 1)

                def own(step):
                    act.wait_ge(pre_act, b * len(PRE_ACT) + PRE_ACT.index(step) + 1)

                dve("center")
                nc.scalar.activation(pre[:, 512:768], pre[:, 256:512], ACT.Square).then_inc(pre_act, 1)
                dve("var")
                nc.scalar.activation(lnt[:, 2, :], lnt[:, 3, :], ACT.Ln).then_inc(pre_act, 1)
                own("ln")
                nc.scalar.activation(lnt[:, 4, :], lnt[:, 2, :], ACT.Exp, scale=-0.5).then_inc(pre_act, 1)
                dve("q_neg")
                nc.scalar.activation(pre[:, 1536:1792], pre[:, 1536:1792], ACT.Exp).then_inc(pre_act, 1)
                dve("k_neg")
                nc.scalar.activation(pre[:, 1792:2048], pre[:, 1792:2048], ACT.Exp).then_inc(pre_act, 1)
                act.wait_ge(pre_pe, (b + 1) * len(PRE_PE))
                nc.scalar.activation(s_out[:, columns(b)], ps_f[:, 0:TOKENS], ACT.Identity,
                                     bias=bp_sb).then_inc(pre_act, 1)

            def copy(o, i):
                return nc.scalar.copy(o, i)

            def squares_of(u, i, s):
                wait(act, ssq_done, 2 * (u - 2) + i + 1)
                act.wait_ge((q_scaled, k_scaled)[i], u + 1)
                nc.scalar.activation(squares[:, s, OCTET * i:OCTET * i + OCTET], (ps_q, ps_k)[i][:], ACT.Square
                                     ).then_inc((q_squared, k_squared)[i], 1)

            def keep_v(u, j):
                wait(act, o_done, u - 2)
                act.wait_ge(v_done, u + 1)
                copy(v_own[:, j, :], ps_v[:]).then_inc(v_copied, 1)

            def keep_turned(u, j, s):
                octet, tile = j // 2, j % 2
                wait(act, s_done, u - 1)
                act.wait_ge(tq_done, u + 1)
                for h in range(2):
                    rows = slice(64 * h, 64 * h + 64)
                    last = copy(q_bd[rows, s, :, h, :], ps_qs[rows, :].rearrange("p (g q) -> p g q", q=WINDOW))
                last.then_inc(q_turned, 1)
                act.wait_ge(tk_done, u + 1)
                copy(k_t[:, octet, :, WINDOW + P * tile:WINDOW + P * tile + P],
                     ps_tk[:].rearrange("p (c t) -> p c t", t=P)).then_inc(k_turned, 1)

            def keep_p(u, s):
                wait(act, o_done, u - 1)
                act.wait_ge(pt_done, u + 1)
                for h in range(2):
                    rows = slice(64 * h, 64 * h + 64)
                    last = copy(p_bd[rows, s, :, h, :], ps_po[rows, :].rearrange("p (g q) -> p g q", q=WINDOW))
                last.then_inc(p_turned, 1)

            def start_norms(u, s):
                act.wait_ge(ssq_clamped, u + 1)
                nc.scalar.activation(ssq_ln[:, s, :], ssq_c[:, s, :], ACT.Ln).then_inc(ssq_logged, 1)
                act.wait_ge(ssq_logged, u + 1)
                nc.scalar.activation(rn_0[:, s, :], ssq_ln[:, s, :], ACT.Exp, scale=-0.5).then_inc(rn_started, 1)

            def keep_attention(u, m, j):
                octet, tile = j // 2, j % 2
                wait(act, (wo_half_done, wo_done)[octet], m)
                act.wait_ge(o_done, u + 1)
                copy(attn_t[:, PAIRS * octet:PAIRS * octet + PAIRS, P * tile:P * tile + P],
                     ps_po[:].rearrange("p (c t) -> p c t", t=P)).then_inc(attn_copied, 1)

            def ln_square(m):
                act.wait_ge(centered, m + 1)
                nc.scalar.activation(lnt[:, 0, :], xc[:], ACT.Square).then_inc(ln_squared, 1)

            def ln_start(m):
                act.wait_ge(var_ready, m + 1)
                nc.scalar.activation(lnt[:, 2, :], lnt[:, 1, :], ACT.Ln, scale=-2.0).then_inc(ln_logged, 1)
                act.wait_ge(ln_logged, m + 1)
                nc.scalar.activation(lnt[:, 3, :], lnt[:, 2, :], ACT.Exp, scale=-0.5).then_inc(ln_started, 1)

            def ff_copy(m, i):
                rows = FF_ROWS[i]
                act.wait_ge(ff1_done, FF_N * m + i + 1)
                if i == 0:
                    wait(act, ff2_done, m)
                    act.wait_ge(w1_loaded, m // BATCHES * 32 + 32)
                nc.scalar.activation(ff_a[0:rows, i, :], ps_f[0:rows, 0:TOKENS], ACT.Identity,
                                     bias=b1_sb[0:rows, i:i + 1])
                nc.scalar.activation(ff_g[0:rows, i, :], ps_f[0:rows, TOKENS:2 * TOKENS], ACT.Identity,
                                     bias=b1_sb[0:rows, FF_N + i:FF_N + i + 1]).then_inc(ff1_copied, 1)

            def gelu(m):
                act.wait_ge(ff1_copied, FF_N * (m + 1))
                nc.scalar.activation(ff_g[:].rearrange("p a b -> p (a b)"),
                                     ff_g[:].rearrange("p a b -> p (a b)"), ACT.Gelu).then_inc(gelu_done, 1)

            def silu_start(b):
                act.wait_ge(x_ready, STEPS + b + 1)
                nc.scalar.activation(silu_e[:, columns(b)], x_run[:, columns(b)],
                                     ACT.Exp, scale=-1.0).then_inc(silu_exp, 1)

            def body(n):
                for j in range(UNITS):
                    u = UNITS * n + j
                    if live(u - 1):
                        keep_turned(u - 1, (j - 1) % UNITS, (j - 1) % 2)
                    if live(u):
                        squares_of(u, 0, j % 2)
                        squares_of(u, 1, j % 2)
                    if j == 0 and live_batch(n - 2):
                        ln_square(n - 2)
                    if live(u - 2):
                        keep_p(u - 2, j % 2)
                    if j == 1 and live_batch(n - 3):
                        nc.scalar.preload_act_table_set("natural_log_exp_and_others")
                    if live(u):
                        start_norms(u, j % 2)
                    if j == 0 and live_batch(n - 3):
                        ff_copy(n - 3, 2)
                    if j >= 2 and live_batch(n - 2):
                        ff_copy(n - 2, j - 2)
                    if j == 1 and live_batch(n - 2):
                        ln_start(n - 2)
                    if live(u - 1):
                        act.wait_ge(sub_done, u)
                        nc.scalar.activation(prob[:, (j - 1) % 2, :], prob[:, (j - 1) % 2, :], ACT.Exp,
                                             scale=QK_SCALE).then_inc(exp_done, 1)
                    if live(u):
                        keep_v(u, j)
                    if live(u - 2):
                        keep_attention(u - 2, n if j >= 2 else n - 1, (j - 2) % UNITS)
                    if j == 0 and live_batch(n - 3):
                        gelu(n - 3)
                    for b in silu_at(n, j):
                        silu_start(b)

            iterations(act, body)

        @block.vector
        def _(dve):
            V = nc.vector
            V.memset(mean_w[:], 1.0 / P)
            V.memset(ones, 1.0)
            V.memset(xs_hi[64:P, 0:1].bitcast(F32), 0.0)
            V.memset(xs_lo[64:P, 0:1].bitcast(F32), 0.0)
            V.memset(xs[64:P, 0:1], 0.0).then_inc(memset_done, 1)
            dve.wait_ge(consts_loaded, 16 * 13)
            V.tensor_copy(ident_b[:], ident[:])
            V.tensor_copy(mask_b[:].rearrange("p a b -> p (a b)"), mask_f).then_inc(consts_ready, 1)

            dve.wait_ge(x_loaded, 16 * BATCHES)
            with dve.Fori(0, BATCHES) as b:
                def step(name, ins):
                    ins.then_inc(pre_dve, 1)

                def own(name):
                    dve.wait_ge(pre_dve, b * len(PRE_DVE) + PRE_DVE.index(name) + 1)

                def pe(name):
                    dve.wait_ge(pre_pe, b * len(PRE_PE) + PRE_PE.index(name) + 1)

                def act(name):
                    dve.wait_ge(pre_act, b * len(PRE_ACT) + PRE_ACT.index(name) + 1)

                xn_b, xc_b = pre[:, 0:256], pre[:, 256:512]
                q_f, k_f, v_f = pre[:, 768:1024], pre[:, 1024:1280], pre[:, 1280:1536]
                q_e, k_e = pre[:, 1536:1792], pre[:, 1792:2048]
                kv = ps_tk[:].rearrange("p (t c) -> p t c", t=TILES)

                def tiled(t):
                    return t.rearrange("p (t c) -> p t c", t=TILES)

                var, r0 = lnt[:, 3, :], lnt[:, 4, :]
                pe("mean")
                step("center", V.tensor_tensor(xc_b, x_in[:, columns(b)], ps_q[:, 0:TOKENS], ALU.subtract))
                pe("var")
                step("var", V.tensor_scalar(var, ps_k[:, 0:TOKENS], LN_EPS, None, ALU.add))
                act("rsqrt")
                own("var")
                step("newton_a", V.scalar_tensor_tensor(out=lnt[:, 2, :], in0=var, scalar=-0.5, in1=r0,
                                                        op0=ALU.mult, op1=ALU.mult))
                own("newton_a")
                step("newton_b", V.tensor_tensor(lnt[:, 5, :], lnt[:, 2, :], r0, ALU.mult))
                own("newton_b")
                step("rstd", V.scalar_tensor_tensor(out=lnt[:, 2, :], in0=lnt[:, 5, :], scalar=1.5, in1=r0,
                                                    op0=ALU.add, op1=ALU.mult))
                own("rstd")
                step("xn", V.tensor_tensor(xn_b, xc_b, lnt[:, 2, :], ALU.mult))
                own("xn")
                step("keep", V.tensor_copy(x_run[:, columns(b)], xn_b))
                pe("qkv")
                step("q_neg", V.tensor_scalar(q_e, ps_qs[:, 0:TOKENS], 0.0, None, ALU.min))
                step("k_neg", V.tensor_scalar(tiled(k_e), kv[:, :, 0:P], 0.0, None, ALU.min))
                step("v_copy", V.tensor_copy(tiled(v_f), kv[:, :, P:2 * P]))
                mix = lnt[:, 2, :]
                step("conv_mid", V.tensor_scalar(mix, xn_b, conv_sb[:, 1:2], convb_sb, ALU.mult, ALU.add))
                own("conv_mid")
                step("conv_left", V.scalar_tensor_tensor(out=mix[:, 1:TOKENS], in0=xn_b[:, 0:TOKENS - 1],
                                                         scalar=conv_sb[:, 0:1], in1=mix[:, 1:TOKENS],
                                                         op0=ALU.mult, op1=ALU.add))
                own("conv_left")
                step("conv_right", V.scalar_tensor_tensor(out=mix[:, 0:TOKENS - 1], in0=xn_b[:, 1:TOKENS],
                                                          scalar=conv_sb[:, 2:3], in1=mix[:, 0:TOKENS - 1],
                                                          op0=ALU.mult, op1=ALU.add))
                act("q_exp")
                step("q_feat", V.scalar_tensor_tensor(out=q_f, in0=ps_qs[:, 0:TOKENS], scalar=0.0, in1=q_e,
                                                      op0=ALU.max, op1=ALU.add))
                act("k_exp")
                step("k_feat", V.scalar_tensor_tensor(out=tiled(k_f), in0=kv[:, :, 0:P], scalar=0.0, in1=tiled(k_e),
                                                      op0=ALU.max, op1=ALU.add))
                pe("state")
                step("kv_state", V.tensor_tensor(lnt[:, 0, 0:P], ps_v[:, 0:P], block_sb, ALU.mult))
                step("k_state", V.tensor_tensor(lnt[:, 1, 0:P], ps_v[:, P:2 * P], block_sb, ALU.mult))
                pe("read")
                step("den", V.tensor_scalar(lnt[:, 3, :], ps_a[:, TOKENS:2 * TOKENS], 1e-6, None, ALU.max))
                own("den")
                step("den_inv", V.reciprocal(lnt[:, 4, :], lnt[:, 3, :]))
                own("den_inv")
                step("attn", V.tensor_tensor(lnt[:, 3, :], ps_a[:, 0:TOKENS], lnt[:, 4, :], ALU.mult))
                own("attn")
                own("conv_right")
                step("mix", V.tensor_tensor(lnt[:, 5, :], lnt[:, 3, :], mix, ALU.add))
                dve.wait_ge(pre_act, (b + 1) * len(PRE_ACT))
            V.sem_inc(x_ready, BATCHES)

            def heads(t):
                return t.rearrange("p (h d) -> p h d", d=HEAD)

            def halves(t):
                return t.rearrange("p (h a c) -> p h a c", a=2, c=HEAD // 2)

            def round_x(n):
                dve.wait_ge(x_ready, n + 1)
                wait(dve, v_done, UNITS * n)
                b = n % BATCHES * TOKENS
                low, high = slice(0, TOKENS), slice(1, TOKENS)
                V.tensor_copy(xs_hi[0:64, low], x_run[0:64, span(b, TOKENS)])
                V.tensor_copy(xs_hi[64:P, high], x_run[64:P, span(b, TOKENS - 1)]).then_inc(xs_rounded, 1)
                dve.wait_ge(xs_rounded, n + 1)
                V.tensor_tensor(xs_lo[0:64, low], x_run[0:64, span(b, TOKENS)], xs_hi[0:64, low].bitcast(F32), ALU.subtract)
                V.tensor_tensor(xs_lo[64:P, high], x_run[64:P, span(b, TOKENS - 1)],
                                xs_hi[64:P, high].bitcast(F32), ALU.subtract).then_inc(xs_ready, 1)

            def rotate(n, j):
                u = UNITS * n + j
                s = j % 2
                tile = j % 2
                wait(dve, tk_done, u - 1)
                for i, ps, done, scaled, added in ((0, ps_q, q_done, q_scaled, q_added),
                                                   (1, ps_k, k_done, k_scaled, k_added)):
                    wait(dve, added, u - 1)
                    dve.wait_ge(done, u + 1)
                    at = n // BATCHES * (4 * TILES * HEAD) + (2 * i * TILES + tile) * HEAD
                    cos = table[:, span(at, HEAD)]
                    sin = table[:, span(at + TILES * HEAD, HEAD)]
                    V.tensor_tensor(heads(qk[:, s, i, :]), heads(ps[:]),
                                    cos.unsqueeze(1).to_broadcast([P, 8, HEAD]), ALU.mult)
                    V.tensor_tensor(halves(qk_rot[:, s, i, :]), halves(ps[:])[:, :, ::-1, :],
                                    sin.rearrange("p (a c) -> p a c", a=2).unsqueeze(1).to_broadcast([P, 8, 2, HEAD // 2]),
                                    ALU.mult).then_inc(scaled, 1)

            def sum_squares(u, i, s):
                dve.wait_ge((q_squared, k_squared)[i], u + 1)
                V.tensor_reduce(ssq[:, s, 8 * i:8 * i + 8], heads(squares[:, s, OCTET * i:OCTET * i + OCTET]), AX,
                                ALU.add).then_inc(ssq_done, 1)

            def clamp(u, s):
                dve.wait_ge(ssq_done, 2 * u + 2)
                V.tensor_scalar(ssq_c[:, s, :], ssq[:, s, :], 1e-24, SQ_SCALE, ALU.max, ALU.mult).then_inc(ssq_clamped, 1)

            def newton_1(u, s):
                dve.wait_ge(rn_started, u + 1)
                V.scalar_tensor_tensor(out=rn_a[:, s, :], in0=ssq_c[:, s, :], scalar=-0.5, in1=rn_0[:, s, :],
                                       op0=ALU.mult, op1=ALU.mult).then_inc(rn_step, 1)

            def newton_2(u, s):
                dve.wait_ge(rn_step, 2 * u + 1)
                V.tensor_tensor(rn_b[:, s, :], rn_a[:, s, :], rn_0[:, s, :], ALU.mult).then_inc(rn_step, 1)

            def newton_3(u, s):
                dve.wait_ge(rn_step, 2 * u + 2)
                wait(dve, k_normed, u - 1)
                V.scalar_tensor_tensor(out=rnorm[:, s, :], in0=rn_b[:, s, :], scalar=1.5, in1=rn_0[:, s, :],
                                       op0=ALU.add, op1=ALU.mult).then_inc(rnorm_done, 1)

            def find_max(u, s):
                dve.wait_ge(s_done, u + 1)
                V.tensor_reduce(row_max[:, s, :], heads(ps_qs[:]), AX, ALU.max).then_inc(max_done, 1)

            def less_max(u, s):
                dve.wait_ge(max_done, u + 1)
                wait(dve, pt_done, u - 1)
                V.tensor_tensor(heads(prob[:, s, :]), heads(ps_qs[:]),
                                row_max[:, s, :].unsqueeze(2).to_broadcast([P, 8, HEAD]),
                                ALU.subtract).then_inc(sub_done, 1)

            def sums(u, s):
                dve.wait_ge(exp_done, u + 1)
                V.tensor_reduce(row_sum[:, s, :], heads(prob[:, s, :]), AX, ALU.add).then_inc(sum_done, 1)
                dve.wait_ge(sum_done, u + 1)
                wait(dve, p_normed, u - 1)
                V.reciprocal(row_inv[:, s, :], row_sum[:, s, :]).then_inc(inv_done, 1)

            def after_attention(m):
                dve.wait_ge(wo_done, m + 1)
                b = m % BATCHES * TOKENS
                V.tensor_tensor(xs[0:64, :], x_run[0:64, span(b, TOKENS)], ps_a[0:64, 0:TOKENS],
                                ALU.add).then_inc(xs_shifted, 1)
                V.tensor_tensor(xs[64:P, 1:TOKENS], x_run[64:P, span(b, TOKENS - 1)], ps_a[64:P, 0:TOKENS - 1],
                                ALU.add).then_inc(xs_shifted, 1)

            def keep_mid(m):
                V.tensor_tensor(x_mid[:, span(m % 2 * TOKENS, TOKENS)], x_run[:, columns(m)],
                                ps_a[:, 0:TOKENS], ALU.add).then_inc(mid_done, 1)

            def ln_center(m):
                dve.wait_ge(mean_done, m + 1)
                dve.wait_ge(xs_shifted, 2 * m + 2)
                V.tensor_tensor(xc[:], xs[:], ps_a[:, TOKENS:2 * TOKENS], ALU.subtract).then_inc(centered, 1)

            def ln_var(m):
                dve.wait_ge(var_done, m + 1)
                V.tensor_scalar(lnt[:, 1, :], ps_f[:, 0:TOKENS], LN_EPS, -0.5, ALU.add, ALU.mult).then_inc(var_ready, 1)

            def ln_refine(m):
                dve.wait_ge(ln_started, m + 1)
                r0 = lnt[:, 3, :]
                V.tensor_tensor(lnt[:, 4, :], lnt[:, 1, :], r0, ALU.mult).then_inc(ln_step, 1)
                V.tensor_tensor(xc[:], xc[:], r0, ALU.mult).then_inc(ln_step, 1)
                dve.wait_ge(ln_step, 4 * m + 1)
                V.tensor_tensor(lnt[:, 5, :], lnt[:, 4, :], r0, ALU.mult).then_inc(ln_step, 1)

            def ln_normalise(m):
                dve.wait_ge(ln_step, 4 * m + 3)
                V.scalar_tensor_tensor(out=lnt[:, 4, :], in0=lnt[:, 5, :], scalar=1.5, in1=xc[:],
                                       op0=ALU.add, op1=ALU.mult).then_inc(ln_step, 1)

            def ln_scale(m):
                dve.wait_ge(ln_step, 4 * m + 4)
                wait(dve, ff1_done, FF_N * m)
                dve.wait_ge(ln_loaded, m // BATCHES * 32 + 32)
                V.tensor_scalar(xn[:], lnt[:, 4, :], ln_sb[:, 0:1], ln_sb[:, 1:2], ALU.mult, ALU.add).then_inc(xn_ready, 1)

            def after_ff(m):
                dve.wait_ge(ff2_done, m + 1)
                dve.wait_ge(w2_loaded, m // BATCHES * 32 + 32)
                V.scalar_tensor_tensor(out=x_run[:, columns(m)], in0=ps_f[:, 0:TOKENS], scalar=b2_sb[:, 0:1],
                                       in1=x_mid[:, span(m % 2 * TOKENS, TOKENS)], op0=ALU.add, op1=ALU.add).then_inc(x_ready, 1)

            def silu(b):
                c = columns(b)
                e = silu_e[:, c]
                dve.wait_ge(silu_exp, b + 1)
                V.tensor_scalar(e, e, 1.0, None, ALU.add).then_inc(final_step, 1)
                dve.wait_ge(final_step, 4 * b + 1)
                V.reciprocal(e, e).then_inc(final_step, 1)
                dve.wait_ge(final_step, 4 * b + 2)
                V.tensor_tensor(e, e, x_run[:, c], ALU.mult).then_inc(final_step, 1)
                dve.wait_ge(final_step, 4 * b + 3)
                V.tensor_tensor(e, e, s_out[:, c], ALU.mult).then_inc(final_step, 1)
                dve.wait_ge(final_step, 4 * b + 4)
                V.tensor_tensor(s_out[:, c], e, x_in[:, c], ALU.add).then_inc(final, 1)

            def body(n):
                for j in range(UNITS):
                    u = UNITS * n + j
                    if live(u):
                        rotate(n, j)
                    if j == 0 and live_batch(n - 2):
                        ln_center(n - 2)
                    if j == 2 and live_batch(n - 3):
                        after_ff(n - 3)
                    if j == 2 and live_batch(n - 2):
                        ln_scale(n - 2)
                    if j == 3 and live(UNITS * (n + 1)):
                        round_x(n + 1)
                    if live(u):
                        sum_squares(u, 0, j % 2)
                        sum_squares(u, 1, j % 2)
                    if j == 0 and live_batch(n - 2):
                        keep_mid(n - 2)
                    if j == 1 and live_batch(n - 2):
                        ln_var(n - 2)
                    if live(u):
                        clamp(u, j % 2)
                    if live(u - 1):
                        find_max(u - 1, (j - 1) % 2)
                    if live(u):
                        newton_1(u, j % 2)
                    if j == 3 and live_batch(n - 1):
                        after_attention(n - 1)
                    if live(u - 1):
                        less_max(u - 1, (j - 1) % 2)
                    if live(u):
                        newton_2(u, j % 2)
                        newton_3(u, j % 2)
                    if j == 1 and live_batch(n - 2):
                        ln_refine(n - 2)
                    if live(u - 1):
                        sums(u - 1, (j - 1) % 2)
                    if j == 1 and live_batch(n - 2):
                        ln_normalise(n - 2)
                    for b in silu_at(n, j):
                        silu(b)

            round_x(0)
            dve.wait_ge(zeros_ready, 1)
            dve.wait_ge(table_ready, 1)
            iterations(dve, body)


def rotary_tables():
    f = np.float32
    half = np.arange(0, HEAD, 2, dtype=f)
    inv_freq = f(1.0) / np.power(f(10000.0), half / f(HEAD))
    t = np.arange(TOKENS, dtype=f)
    freqs = t[:, None] * inv_freq[None, :]
    base = (half + f(0.4 * HEAD)) / f(1.4 * HEAD)
    power = (t - f(TOKENS // 2)) / f(WINDOW // 2)
    scale = np.power(base[None, :], power[:, None])
    cos, sin = np.cos(freqs), np.sin(freqs)
    both = []
    for sc in (scale, f(1.0) / scale):
        both.append(np.concatenate([cos * sc, cos * sc], -1))
        both.append(np.concatenate([-sin * sc, sin * sc], -1))
    tab = np.stack(both) * f(SQ_SCALE ** 0.5)
    return np.ascontiguousarray(tab.reshape(4, TILES, P, HEAD).transpose(2, 0, 1, 3).reshape(P, -1).astype(f))


def score_masks():
    q = np.arange(WINDOW)[:, None]
    k = np.arange(WINDOW)[None, :]
    seen = np.concatenate([k >= q, k <= q], 1)
    m = np.where(seen, 0.0, MASKED)[None, None, :, None, None, None, :]
    m = np.broadcast_to(m, (2, 2, WINDOW, TILES, PAIRS, 2, 2 * WINDOW)).copy()
    m[0, :, :, 0, :, 0, 0:WINDOW] = MASKED
    return m.reshape(P, TILES * 512).astype(np.float32)


def kernel(**inputs):
    import concourse.bacc as bacc
    from concourse.bass_utils import run_bass_kernel_spmd

    a = {k.replace("L0_", ""): np.asarray(v) for k, v in inputs.items()}
    def turned(w):
        return np.ascontiguousarray(w.T)

    b1 = np.zeros((DEPTH, P, 2 * FF_N), np.float32)
    w2 = np.zeros((DEPTH, P, FF_N, DIM), np.float32)
    for i, rows in enumerate(FF_ROWS):
        b1[:, 0:rows, i] = a["ffn_b1"][:, P * i:P * i + rows]
        b1[:, 0:rows, FF_N + i] = a["ffn_b1"][:, FF + P * i:FF + P * i + rows]
        w2[:, 0:rows, i] = a["ffn_W2"][:, P * i:P * i + rows]
    arrays = {
        "x": turned(a["attn_x"].reshape(ALL, DIM)),
        "wq": turned(a["attn_Wq"]), "wk": turned(a["attn_Wk"]), "wv": turned(a["attn_Wv"]), "wp": turned(a["attn_Wp"]),
        "bp": a["attn_bp"].reshape(DIM, 1), "conv_w": a["attn_conv_w"], "conv_b": a["attn_conv_b"].reshape(DIM, 1),
        "wqkv": a["ffn_Wqkv"].reshape(DEPTH, DIM, SLICES, SLICE).transpose(0, 2, 1, 3).reshape(DEPTH * SLICES, DIM, SLICE),
        "q_scale": a["ffn_q_scale"].reshape(-1), "k_scale": a["ffn_k_scale"].reshape(-1),
        "wo": a["ffn_Wo"].reshape(DEPTH, CHUNKS, P, DIM).transpose(0, 2, 1, 3).reshape(DEPTH, P, CHUNKS * DIM),
        "ln_g": a["ffn_ln_g"].reshape(DEPTH, DIM, 1), "ln_b": a["ffn_ln_b"].reshape(DEPTH, DIM, 1),
        "w1": a["ffn_W1"], "b1": b1, "w2": w2.reshape(DEPTH, P, FF_N * DIM), "b2": a["ffn_b2"].reshape(DEPTH, DIM, 1),
        "rotary": rotary_tables(), "masks": score_masks(), "eye": np.eye(P, dtype=np.float32),
        "head_block": np.kron(np.eye(HEADS), np.ones((LINEAR_HEAD, LINEAR_HEAD))).astype(np.float32),
    }
    arrays = {k: np.ascontiguousarray(v) for k, v in arrays.items()}
    nc = bacc.Bacc("TRN2", target_bir_lowering=False, num_devices=1)
    aps = [nc.dram_tensor("in_" + k, v.shape, mybir.dt.from_np(v.dtype), kind="ExternalInput").ap()
           for k, v in arrays.items()]
    out = nc.dram_tensor("out", (P, ALL), F32, kind="ExternalOutput").ap()
    build(nc, *aps, out)
    r = run_bass_kernel_spmd(nc, [{"in_" + k: v for k, v in arrays.items()}], core_ids=[0])
    y = np.asarray(r.results[0]["out"])
    return np.ascontiguousarray(y.T).reshape(BATCHES, TOKENS, DIM)
```
